# Optimizing a Trainium2 kernel written in Bass

```python
import numpy as np
import jax
import jax.numpy as jnp

def _softmax(x, axis=-1):
    return jax.nn.softmax(x, axis=axis)

def _gelu(x):
    return jax.nn.gelu(x, approximate=True)

def _silu(x):
    return jax.nn.silu(x)

def _sigmoid(x):
    return jax.nn.sigmoid(x)

def _layernorm(x, axis=-1, eps=1e-05):
    m = jnp.mean(x, axis=axis, keepdims=True)
    v = jnp.var(x, axis=axis, keepdims=True)
    return (x - m) / jnp.sqrt(v + eps)

def _scatter_add(tgt, idx, src, axis=0):
    return tgt.at[idx].add(src)

def _segment_sum(src, seg, n):
    return jax.ops.segment_sum(src, seg, n)
kernel_name = 'mk_prb_d1_jaxref_r8_52fa06'

def setup_inputs(seed: int=0):
    np.random.seed(seed)
    _w = jnp.asarray

    def _L0_attn_setup():
        import jax, jax.numpy as jnp
        import numpy as np
        BATCH, SEQ, EMBED = (8, 128, 256)
        HEADS, LATENT = (16, 64)
        HEAD_DIM = EMBED // HEADS
        NOPE = HEAD_DIM // 4
        ROPE_D = HEAD_DIM - NOPE
        THETA = 10000.0

        def _rope_tables(seq_len):
            freqs = 1.0 / THETA ** (jnp.arange(0, ROPE_D, 2, dtype=jnp.float32) / ROPE_D)
            emb = jnp.arange(seq_len, dtype=jnp.float32)[:, None] * freqs[None, :]
            return (jnp.cos(emb), jnp.sin(emb))

        def _apply_rope(x, cos, sin):
            xe, xo = (x[..., ::2], x[..., 1::2])
            return jnp.concatenate([xe * cos - xo * sin, xo * cos + xe * sin], axis=-1)
        key = jax.random.key(seed)
        ks = jax.random.split(key, 5)
        x = jax.random.normal(ks[0], (BATCH, SEQ, EMBED), jnp.float32)
        Wq = jax.random.normal(ks[1], (EMBED, EMBED), jnp.float32) * 0.02
        Wkv_down = jax.random.normal(ks[2], (EMBED, LATENT), jnp.float32) * 0.02
        Wk_up = jax.random.normal(ks[3], (LATENT, EMBED), jnp.float32) * 0.02
        Wv_up = jax.random.normal(ks[4], (LATENT, EMBED), jnp.float32) * 0.02
        return {'x': x, 'Wq': Wq, 'Wkv_down': Wkv_down, 'Wk_up': Wk_up, 'Wv_up': Wv_up}
    _L0_attn_in = _L0_attn_setup()

    def _L0_ffn_setup():
        import jax, jax.numpy as jnp
        import numpy as np
        BLOCK = 128
        MAXVAL = 448.0

        def _quant_dequant(x_flat):
            xb = x_flat.reshape(-1, BLOCK)
            s = jnp.max(jnp.abs(xb), axis=1, keepdims=True) / MAXVAL
            q = (xb / s).astype(jnp.float8_e4m3fn)
            return (q.astype(jnp.float32) * s).reshape(x_flat.shape)
        key = jax.random.key(seed)
        k1, k2 = jax.random.split(key)
        B, T, D, OUT = (4, 512, 256, 256)
        x = jax.random.normal(k1, (B, T, D), dtype=jnp.float32)
        limit = float(np.sqrt(6.0 / (D + OUT)))
        weight = jax.random.uniform(k2, (OUT, D), minval=-limit, maxval=limit, dtype=jnp.float32)
        return {'x': x, 'weight': weight}
    _L0_ffn_in = _L0_ffn_setup()
    _d = {'L0_attn_x': _L0_attn_in['x'], 'L0_attn_Wq': _L0_attn_in['Wq'], 'L0_attn_Wkv_down': _L0_attn_in['Wkv_down'], 'L0_attn_Wk_up': _L0_attn_in['Wk_up'], 'L0_attn_Wv_up': _L0_attn_in['Wv_up'], 'L0_ffn_weight': _L0_ffn_in['weight']}
    _x0 = _d['L0_attn_x']
    _d['L0_attn_x'] = jax.random.normal(jax.random.fold_in(jax.random.key(seed), 1), (2, 1024, 256), dtype=_x0.dtype)
    del _x0
    return _d

def reference(L0_attn_x, L0_attn_Wq, L0_attn_Wkv_down, L0_attn_Wk_up, L0_attn_Wv_up, L0_ffn_weight):

    def _L0_attn_ref(x, Wq, Wkv_down, Wk_up, Wv_up):
        import jax, jax.numpy as jnp
        import numpy as np
        BATCH, SEQ, EMBED = (8, 128, 256)
        HEADS, LATENT = (16, 64)
        HEAD_DIM = EMBED // HEADS
        NOPE = HEAD_DIM // 4
        ROPE_D = HEAD_DIM - NOPE
        THETA = 10000.0

        def _rope_tables(seq_len):
            freqs = 1.0 / THETA ** (jnp.arange(0, ROPE_D, 2, dtype=jnp.float32) / ROPE_D)
            emb = jnp.arange(seq_len, dtype=jnp.float32)[:, None] * freqs[None, :]
            return (jnp.cos(emb), jnp.sin(emb))

        def _apply_rope(x, cos, sin):
            xe, xo = (x[..., ::2], x[..., 1::2])
            return jnp.concatenate([xe * cos - xo * sin, xo * cos + xe * sin], axis=-1)
        B, S, E = x.shape
        q = (x @ Wq).reshape(B, S, HEADS, HEAD_DIM).transpose(0, 2, 1, 3)
        q_nope, q_rope = (q[..., :NOPE], q[..., NOPE:])
        c_kv = x @ Wkv_down
        k = (c_kv @ Wk_up).reshape(B, S, HEADS, HEAD_DIM).transpose(0, 2, 1, 3)
        v = (c_kv @ Wv_up).reshape(B, S, HEADS, HEAD_DIM).transpose(0, 2, 1, 3)
        k_nope, k_rope = (k[..., :NOPE], k[..., NOPE:])
        cos, sin = _rope_tables(S)
        q_rope = _apply_rope(q_rope, cos, sin)
        k_rope = _apply_rope(k_rope, cos, sin)
        qf = jnp.concatenate([q_nope, q_rope], axis=-1)
        kf = jnp.concatenate([k_nope, k_rope], axis=-1)
        scale = jnp.float32(1.0 / np.sqrt(HEAD_DIM))
        scores = jnp.einsum('bhqd,bhkd->bhqk', qf, kf) * scale
        causal = jnp.triu(jnp.ones((S, S), dtype=bool), k=1)
        scores = jnp.where(causal, -jnp.inf, scores)
        weights = jax.nn.softmax(scores, axis=-1)
        out = jnp.einsum('bhqk,bhkd->bhqd', weights, v)
        return out.transpose(0, 2, 1, 3).reshape(B, S, E)

    def _L0_ffn_ref(x, weight):
        import jax, jax.numpy as jnp
        import numpy as np
        BLOCK = 128
        MAXVAL = 448.0

        def _quant_dequant(x_flat):
            xb = x_flat.reshape(-1, BLOCK)
            s = jnp.max(jnp.abs(xb), axis=1, keepdims=True) / MAXVAL
            q = (xb / s).astype(jnp.float8_e4m3fn)
            return (q.astype(jnp.float32) * s).reshape(x_flat.shape)
        B, T, D = x.shape
        x_deq = _quant_dequant(x.reshape(-1)).reshape(B * T, D)
        w_deq = _quant_dequant(weight.reshape(-1)).reshape(weight.shape)
        out = x_deq @ w_deq.T
        return out.reshape(B, T, -1)
    x = L0_attn_x
    xn = _layernorm(x, axis=-1)
    x = x + _L0_attn_ref(xn, L0_attn_Wq, L0_attn_Wkv_down, L0_attn_Wk_up, L0_attn_Wv_up) + _L0_ffn_ref(xn, L0_ffn_weight)
    return x

_drawn_inputs = setup_inputs


def setup_inputs(seed=0):
    import zlib

    import numpy as np

    out = dict(_drawn_inputs(seed))
    spreads = {}
    factors = {'L0_attn_Wq': 8.0, 'L0_attn_Wkv_down': 8.0, 'L0_attn_Wk_up': 8.0, 'L0_attn_Wv_up': 8.0}
    for name, (base, spread) in spreads.items():
        noise = np.random.default_rng([zlib.crc32(name.encode()), seed]).standard_normal(out[name].shape)
        drawn = base * np.exp(spread * noise) if base else spread * noise
        out[name] = jnp.asarray(drawn.astype(out[name].dtype))
    for name, factor in factors.items():
        out[name] = (out[name] * factor).astype(out[name].dtype)
    return out
```

```python
from contextlib import ExitStack

import concourse.bass as bass
from concourse import mybir

ALU = mybir.AluOpType
ACT = mybir.ActivationFunctionType
AX = mybir.AxisListType
F32 = mybir.dt.float32
BF16 = mybir.dt.bfloat16
U32 = mybir.dt.uint32

P = 128
BATCH, SEQ, EMBED = 2, 1024, 256
HEADS, LATENT = 16, 64
HEAD_DIM = EMBED // HEADS
NOPE = HEAD_DIM // 4
ROPE = HEAD_DIM - NOPE
SCALE = HEAD_DIM ** -0.5
LN_EPS = 1e-5
THETA = 10000.0

TILES = BATCH * SEQ // P
SEQ_TILES = SEQ // P
CHUNK = 512
CT = CHUNK // P
CHUNKS = BATCH * SEQ // CHUNK
CPB = SEQ // CHUNK
HG = 4
GROUPS = BATCH * HEADS // HG
GPB = HEADS // HG
HALF = HEAD_DIM // 2
EH = EMBED // P

PARTS = 3
Q_SLOTS = [0, 0, 0, 1, 1, 2]
K_SLOTS = [0, 1, 2, 0, 1, 0]
SPLIT_ROWS = len(Q_SLOTS) * HEAD_DIM
ALL_ROWS = SPLIT_ROWS + 2
VC = 32

QBLOCK = 128
FP8_MAX = 448.0
FP8_LEAST_NORMAL = 2.0 ** -6
ROUND_3_BITS = 1.5 * 2.0 ** 20
MASKED = -1e30
LOWEST = -3e38
TWO_BF16_ONES = 1.0 + 0x3F80 / 2.0 ** 23

NS, NT, NA = 2, 2, 2
BANKS_S = list(range(NS))
BANKS_T = list(range(NS, NS + NT))
BANKS_O = [NS + NT, NS + NT + 1]
BANKS_A = list(range(NS + NT + 2, NS + NT + 2 + NA))
KQ_SLOTS = 3
PR = 3


def max_units():
    units = [[(h, i, j, 4)] for i, j in ((3, 0), (7, 0), (7, 4), (4, 0), (5, 0), (6, 0)) for h in range(HG)]
    units += [[(h, i, j, 2) for h in (hp, hp + 1)] for i, j in ((1, 0), (2, 0), (5, 4), (6, 4)) for hp in (0, 2)]
    units += [[(h, i, j, 1) for h in range(HG)] for i, j in ((0, 0), (4, 4), (2, 2), (6, 6))]
    return units


QUADS = [
    [(0, 0, 0, 4)],
    [(0, 1, 1, 3), (0, 3, 3, 1)],
    [(1, 0, 4, 4)],
    [(0, 2, 2, 2), (1, 6, 6, 2)],
    [(1, 1, 4, 4)],
    [(1, 2, 4, 4)],
    [(1, 3, 4, 4)],
    [(1, 4, 4, 4)],
    [(1, 5, 5, 3), (1, 7, 7, 1)],
]
UNITS = max_units()
NQ = len(QUADS)
HALF_FIRST = [0, 2]
HALF_LAST = [3, 8]


def diagonals(q):
    out, col = [], 0
    for _, j, q0, n in QUADS[q]:
        if q0 == j:
            out.append(col)
        col += n * P
    return out


DIAGONALS = [diagonals(q) for q in range(NQ)]


def plan():
    def front(c):
        return [[("ln", c), ("xt", c, 0), ("xt", c, 1)], [("ckv", c)],
                [("proj", 0, c), ("rope", 0, c), ("part1", 0, c)],
                [("proj", 1, c), ("rest1", 0, c), ("part2", 0, c), ("part3", 0, c), ("rope", 1, c), ("part1", 1, c)],
                [("v", c, 0), ("rest1", 1, c), ("part2", 1, c), ("part3", 1, c)], [("v", c, 1)]]

    def ffn(c):
        return [[("scale", c)], [("quant", c)], [("round", c)], [("xdt", c, 0)], [("xdt", c, 1)],
                [("ffn", c, 0)], [("ffn", c, 1)]]

    order = [("ln", 0), ("ln", 1)]
    for c in range(CPB):
        for piece in front(c):
            order += [e for e in piece if e[0] != "ln"]
    order += [("load", 0), ("load", 1), ("load", 2)]
    order += [("s", 0, u) for u in range(len(UNITS))] + [("max", 0), ("shift", 0)]
    side = []
    for c in range(CPB, CHUNKS):
        side += front(c)
    side += [[("scale", "w")], [("quant", "w")], [("round", "w")], [("wt",)]]
    for c in range(CHUNKS):
        side += ffn(c)
    for g in range(GROUPS):
        left = list(range(len(UNITS))) if g + 1 < GROUPS else []
        for q in range(NQ):
            for h in range(HG):
                if left:
                    order.append(("s", g + 1, left.pop(0)))
                order.append(("t", g, q, h))
            if left and q % 2 == 0:
                order.append(("s", g + 1, left.pop(0)))
            if DIAGONALS[q]:
                order.append(("diag", g, q))
            if q >= 2:
                order.append(("pv", g, q - 2))
            if q - 2 == HALF_LAST[0]:
                order.append(("oev", g, 0))
            if q == NQ - 2:
                order.append(("ot", g, 0))
                if g + 1 < GROUPS:
                    order.append(("max", g + 1))
            if side:
                order += side.pop(0)
        if g + 1 < GROUPS:
            order.append(("shift", g + 1))
        order += [("pv", g, NQ - 2), ("pv", g, NQ - 1), ("oev", g, 1), ("ot", g, 1)]
        if g + KQ_SLOTS < GROUPS:
            order.append(("load", g + KQ_SLOTS))
        if (g + 1) % GPB == 0:
            order.append(("out", g // GPB))
    assert not side
    return order


def build(nc, x, wq, wkd, wku, wv, wffn, cos, sin, out):
    order = plan()
    at = {e: n for n, e in enumerate(order)}
    assert len(at) == len(order)

    filling, fillings, turn = {}, [0] * 8, {"s": 0, "t": 0, "a": 0}

    def take(key, kind, banks):
        b = banks[turn[kind] % len(banks)]
        turn[kind] += 1
        filling[key] = (b, fillings[b])
        fillings[b] += 1

    for e in order:
        if e[0] == "s":
            take(e, "s", BANKS_S)
        elif e[0] == "t":
            take(e, "t", BANKS_T)
        elif e[0] == "pv":
            for half in range(2):
                if e[2] == HALF_LAST[half]:
                    b = BANKS_O[half]
                    filling["o", e[1], half] = (b, fillings[b])
                    fillings[b] += 1
        elif e[0] == "proj":
            take(e + (0,), "a", BANKS_A)
            take(e + (1,), "a", BANKS_A)
        elif e[0] in ("xt", "ckv", "v", "shift", "ot", "xdt", "ffn", "wt"):
            take(e, "a", BANKS_A)
    ring = {e: n for n, e in enumerate(e for e in order if e[0] == "t")}
    quads = {e[1:3]: n // HG for e, n in ring.items()}
    diag_count = {e[1:]: n + 1 for n, e in enumerate(e for e in order if e[0] == "diag")}
    pv_count = {e[1:]: n + 1 for n, e in enumerate(e for e in order if e[0] == "pv")}
    ot_count = {e[1:]: n + 1 for n, e in enumerate(e for e in order if e[0] == "ot")}
    split_count = {e[1:]: n + 1 for n, e in enumerate(e for e in order if e[0] == "proj")}
    chunk_count = {e[1]: n + 1 for n, e in enumerate(e for e in order if e[0] == "ln")}
    quant_count = {e[1]: n + 1 for n, e in enumerate(e for e in order if e[0] == "scale")}
    ffn_count = {e[1:]: n + 1 for n, e in enumerate(e for e in order if e[0] == "ffn")}
    xdt_count = {e[1:]: n + 1 for n, e in enumerate(e for e in order if e[0] == "xdt")}

    with ExitStack() as ctx:
        def sb(name, shape, dt=F32):
            return ctx.enter_context(nc.sbuf_tensor(name, shape, dt))

        def sem(name):
            return ctx.enter_context(nc.semaphore(name))

        xs = sb("xs", [P, TILES, EMBED])
        wq_sb = sb("wq_sb", [P, EH, EMBED])
        wkd_sb = sb("wkd_sb", [P, EH, LATENT])
        wku_sb = sb("wku_sb", [LATENT, EMBED])
        wv_sb = sb("wv_sb", [LATENT, EMBED])
        w_sb = sb("w_sb", [P, EH, EMBED])
        cos_sb = sb("cos_sb", [P, SEQ])
        sin_sb = sb("sin_sb", [P, SEQ])
        ident = sb("ident", [P, P])
        ident_bf = sb("ident_bf", [P, P], BF16)
        mask_bf = sb("mask_bf", [P, 4, P], BF16)
        stats = sb("stats", [P, CT, 6])
        moments = sb("moments", [P, TILES, 2])
        variance = sb("variance", [P, TILES])
        deviation = sb("deviation", [P, TILES])
        rstd = sb("rstd", [P, TILES])
        newton = sb("newton", [P, TILES])
        xn = sb("xn", [P, TILES, EMBED])
        xnt = sb("xnt", [P, 2, EH, CHUNK])
        ckvt = sb("ckvt", [LATENT, 2, CHUNK])
        rope_products = sb("rope_products", [P, 4, CHUNK])
        rotated = sb("rotated", [P, 2, CHUNK])
        rest = sb("rest", [P, 2, CHUNK])
        parts = sb("parts", [P, 2, PARTS, 2, CHUNK], BF16)
        v_sb = sb("v_sb", [P, BATCH, SEQ_TILES, HEADS, 17])
        qt = sb("qt", [ALL_ROWS, KQ_SLOTS, HG, SEQ], BF16)
        kt = sb("kt", [ALL_ROWS, KQ_SLOTS, HG, SEQ], BF16)
        block_max = sb("block_max", [P, 2, HG, SEQ_TILES, SEQ_TILES])
        neg_max = sb("neg_max", [P, HG * SEQ_TILES])
        shift_parts = sb("shift_parts", [P, 2 * HG * SEQ_TILES], BF16)
        shift_t = sb("shift_t", [2 * HG * SEQ_TILES, P], BF16)
        probs = sb("probs", [P, PR, HG, CHUNK])
        o_sb = sb("o_sb", [P, 2, CHUNK])
        inv_sum = sb("inv_sum", [P, 2, CT, HG])
        attn = sb("attn", [P, 2, CT, HG, HEAD_DIM])
        amax = sb("amax", [P, 8])
        qscale = sb("qscale", [P, 8])
        qinv = sb("qinv", [P, 8])
        qx = sb("qx", [P, 8, QBLOCK])
        qexp = sb("qexp", [P, 8, QBLOCK])
        xdt = sb("xdt", [P, EH, CHUNK])
        wt = sb("wt", [P, EH, EMBED])

        ps = ctx.enter_context(nc.psum_tensor("ps", [P, 8, 512], F32))
        scratch = nc.dram_tensor("split_scratch", [2, BATCH, PARTS, 2, P, SEQ], BF16).ap()

        bank_filled = [sem(f"bank_filled{b}") for b in range(8)]
        bank_drained = [sem(f"bank_drained{b}") for b in range(8)]
        x_loaded = [sem(f"x_loaded{c}") for c in range(CHUNKS)]
        w_loaded = sem("w_loaded")
        wffn_loaded = sem("wffn_loaded")
        tables_loaded = sem("tables_loaded")
        consts_set = sem("consts_set")
        psum_cleared = sem("psum_cleared")
        dve_chain = sem("dve_chain")
        pool_chain = sem("pool_chain")
        var_ready = sem("var_ready")
        dev_ready = sem("dev_ready")
        xn_ready = sem("xn_ready")
        rotated_ready = sem("rotated_ready")
        part1_ready = sem("part1_ready")
        rest_ready = sem("rest_ready")
        part2_ready = sem("part2_ready")
        part3_ready = sem("part3_ready")
        parts_stored = [sem(f"parts_stored{k}") for k in range(2)]
        kq_loaded = [sem(f"kq_loaded{k}") for k in range(KQ_SLOTS)]
        shift_split = sem("shift_split")
        shift_placed = sem("shift_placed")
        probs_zeroed = sem("probs_zeroed")
        pv_done = sem("pv_done")
        attn_added = sem("attn_added")
        scales_ready = sem("scales_ready")
        scaled_ready = sem("scaled_ready")
        exponents_ready = sem("exponents_ready")
        dequantized = sem("dequantized")
        out_stored = sem("out_stored")

        def bank(key):
            return ps[:, filling[key][0], :]

        def wait_filled(eng, key):
            b, n = filling[key]
            eng.wait_ge(bank_filled[b], n + 1)

        def wait_free(eng, key):
            b, n = filling[key]
            if n:
                eng.wait_ge(bank_drained[b], n)

        def wait_drained(eng, key):
            b, n = filling[key]
            eng.wait_ge(bank_drained[b], n + 1)

        def filled(ins, key):
            ins.then_inc(bank_filled[filling[key][0]], 1)

        def drained(ins, key):
            ins.then_inc(bank_drained[filling[key][0]], 1)

        def quant_source(c):
            if c == "w":
                return w_sb[:, :, :].rearrange("p a (k f) -> p (a k) f", f=QBLOCK), EH * EMBED // QBLOCK
            return (xn[:, c * CT:(c + 1) * CT, :].rearrange("p a (k f) -> p (a k) f", f=QBLOCK),
                    CT * EMBED // QBLOCK)

        block = ctx.enter_context(nc.Block())

        @block.sync
        def _(sp):
            xv = x.rearrange("b (t p) e -> p (b t) e", p=P)
            sp.dma_start(xs[:, 0:CT, :], xv[:, 0:CT, :]).then_inc(x_loaded[0], 16)
            sp.dma_start(wkd_sb[:, :, :], wkd.rearrange("(a p) n -> p a n", p=P)).then_inc(w_loaded, 16)
            sp.dma_start(wq_sb[:, :, :], wq.rearrange("(a p) n -> p a n", p=P)).then_inc(w_loaded, 16)
            sp.dma_start(wku_sb[:, :], wku).then_inc(w_loaded, 16)
            sp.dma_start(wv_sb[:, :], wv).then_inc(w_loaded, 16)
            for row in range(HALF):
                for dst, src in ((cos_sb, cos), (sin_sb, sin)):
                    sp.dma_start(dst[row * HEADS:(row + 1) * HEADS, :],
                                 src[row:row + 1, :].partition_broadcast(HEADS)).then_inc(tables_loaded, 16)
            for c in range(1, CHUNKS):
                sp.dma_start(xs[:, c * CT:(c + 1) * CT, :], xv[:, c * CT:(c + 1) * CT, :]).then_inc(x_loaded[c], 16)
            sp.dma_start(w_sb[:, :, :], wffn.rearrange("(a p) n -> p a n", p=P)).then_inc(wffn_loaded, 16)
            outs = 0
            for e in order:
                if e[0] == "part3":
                    _, t, c = e
                    n = split_count[t, c]
                    b, c0 = c // CPB, (c % CPB) * CHUNK
                    sp.wait_ge(part3_ready, n)
                    for part in range(PARTS):
                        sp.dma_start(scratch[t, b, part, :, :, c0:c0 + CHUNK].rearrange("a p n -> p a n"),
                                     parts[:, n % 2, part, :, :]).then_inc(parts_stored[n % 2], 16)
                elif e[0] == "load":
                    g = e[1]
                    b, h0 = g // GPB, (g % GPB) * HG
                    for k in range(2):
                        sp.wait_ge(parts_stored[k], 16 * PARTS * CPB * (b + 1))
                    if g >= KQ_SLOTS:
                        sp.wait_ge(pv_done, pv_count[g - KQ_SLOTS, NQ - 1])
                    for t, (dst, slots) in enumerate(((qt, Q_SLOTS), (kt, K_SLOTS))):
                        rows = scratch[t, b].rearrange("s a (d h) n -> (s a d) (h n)", h=HEADS)
                        for s, part in enumerate(slots):
                            sp.dma_start(dst[s * HEAD_DIM:(s + 1) * HEAD_DIM, g % KQ_SLOTS, :, :]
                                         .rearrange("p h n -> p (h n)"),
                                         rows[part * HEAD_DIM:(part + 1) * HEAD_DIM, h0 * SEQ:(h0 + HG) * SEQ])\
                              .then_inc(kq_loaded[g % KQ_SLOTS], 16)
                elif e[0] == "shift":
                    g = e[1]
                    wait_drained(sp, e)
                    n = HG * SEQ_TILES
                    for part in range(2):
                        row = SPLIT_ROWS + part
                        sp.dma_start(qt[row:row + 1, g % KQ_SLOTS, :, :].rearrange("p h (i n) -> p (h i) n", n=P),
                                     shift_t[part * n:(part + 1) * n, :]).then_inc(shift_placed, 16)
                elif e[0] == "out":
                    b = e[1]
                    sp.wait_ge(attn_added, ot_count[(b + 1) * GPB - 1, 1])
                    sp.dma_start(out[b].rearrange("(t p) e -> p t e", p=P),
                                 xs[:, b * SEQ_TILES:(b + 1) * SEQ_TILES, :]).then_inc(out_stored, 16)
                    outs += 16
            sp.wait_ge(out_stored, outs)

        @block.gpsimd
        def _(pool):
            chain = [0]

            def link(ins):
                chain[0] += 1
                ins.then_inc(pool_chain, 1)
                pool.wait_ge(pool_chain, chain[0])

            nc.gpsimd.memset(ident[:, :], 0.0)
            nc.gpsimd.memset(ident_bf[:, :], 0.0)
            nc.gpsimd.memset(mask_bf[:, :, :], 0.0)
            link(nc.gpsimd.memset(v_sb[:, :, :, :, HEAD_DIM:17], 1.0))
            link(nc.gpsimd.memset(kt[SPLIT_ROWS:ALL_ROWS, :, :, :].rearrange("p a b n -> p (a b n)").bitcast(F32),
                                  TWO_BF16_ONES))
            for m in (ident, ident_bf):
                nc.gpsimd.affine_select(out=m[:, :], in_=m[:, :], compare_op=ALU.not_equal, fill=1.0,
                                        base=0, pattern=[[-1, P]], channel_multiplier=1)
            nc.gpsimd.affine_select(out=mask_bf[:, :, :], in_=mask_bf[:, :, :], compare_op=ALU.is_ge, fill=MASKED,
                                    base=0, pattern=[[0, 4], [-1, P]], channel_multiplier=1).then_inc(consts_set, 1)
            for e in order:
                if e[0] == "rope":
                    n = split_count[e[1:]]
                    wait_drained(pool, ("proj",) + e[1:] + (1,))
                    if n > 1:
                        pool.wait_ge(rest_ready, n - 1)
                    nc.gpsimd.tensor_tensor(rotated[:, 0, :], rope_products[:, 0, :], rope_products[:, 3, :],
                                            ALU.subtract)
                    nc.gpsimd.tensor_tensor(rotated[:, 1, :], rope_products[:, 2, :], rope_products[:, 1, :],
                                            ALU.add).then_inc(rotated_ready, 1)
                elif e[0] == "part3":
                    n = split_count[e[1:]]
                    pool.wait_ge(part2_ready, n)
                    nc.gpsimd.tensor_tensor(parts[:, n % 2, 2, :, :], rest[:, :, :], parts[:, n % 2, 1, :, :],
                                            ALU.subtract).then_inc(part3_ready, 1)
                elif e[0] == "diag":
                    _, g, q = e
                    wait_drained(pool, ("t", g, q, HG - 1))
                    for n, col in enumerate(DIAGONALS[q]):
                        v = probs[:, quads[g, q] % PR, :, col:col + P]
                        ins = nc.gpsimd.affine_select(out=v, in_=v, compare_op=ALU.is_ge, fill=0.0, base=0,
                                                      pattern=[[0, HG], [1, P]], channel_multiplier=-1)
                    ins.then_inc(probs_zeroed, 1)
                elif e[0] == "ot":
                    _, g, half = e
                    b, h0 = g // GPB, (g % GPB) * HG
                    t0 = b * SEQ_TILES + half * CT
                    wait_drained(pool, e)
                    for pair in range(2):
                        key = ("ffn", t0 // CT, pair)
                        if at[key] < at[e]:
                            wait_drained(pool, key)
                    dst = xs[:, t0:t0 + CT, h0 * HEAD_DIM:(h0 + HG) * HEAD_DIM]
                    src = attn[:, half, :, :, :].rearrange("p t h d -> p t (h d)")
                    nc.gpsimd.tensor_tensor(dst, dst, src, ALU.add).then_inc(attn_added, 1)
                elif e[0] == "quant":
                    c = e[1]
                    src, n = quant_source(c)
                    pool.wait_ge(scales_ready, quant_count[c])
                    for key in at:
                        if key[0] in ("xdt", "wt") and at[key] < at[e]:
                            before = key
                    if quant_count[c] > 1:
                        wait_filled(pool, before)
                    nc.gpsimd.tensor_tensor(qx[:, 0:n, :], src,
                                            qinv[:, 0:n].unsqueeze(2).to_broadcast([P, n, QBLOCK]),
                                            ALU.mult).then_inc(scaled_ready, 1)
                elif e[0] == "round":
                    c = e[1]
                    _, n = quant_source(c)
                    pool.wait_ge(exponents_ready, quant_count[c])
                    link(nc.gpsimd.tensor_scalar(qexp[:, 0:n, :], qexp[:, 0:n, :], FP8_LEAST_NORMAL, ROUND_3_BITS,
                                                 ALU.max, ALU.mult))
                    link(nc.gpsimd.tensor_tensor(qx[:, 0:n, :], qx[:, 0:n, :], qexp[:, 0:n, :], ALU.add))
                    link(nc.gpsimd.tensor_tensor(qx[:, 0:n, :], qx[:, 0:n, :], qexp[:, 0:n, :], ALU.subtract))
                    nc.gpsimd.tensor_tensor(qx[:, 0:n, :], qx[:, 0:n, :],
                                            qscale[:, 0:n].unsqueeze(2).to_broadcast([P, n, QBLOCK]),
                                            ALU.mult).then_inc(dequantized, 1)

        @block.scalar
        def _(act):
            for e in order:
                if e[0] == "ln":
                    c = e[1]
                    act.wait_ge(var_ready, chunk_count[c])
                    nc.scalar.activation(deviation[:, c * CT:(c + 1) * CT], variance[:, c * CT:(c + 1) * CT],
                                         ACT.Sqrt).then_inc(dev_ready, 1)
                elif e[0] == "xt":
                    _, c, eh = e
                    wait_filled(act, e)
                    if c >= 2:
                        wait_filled(act, ("proj", 0, c - 2, 1))
                    drained(nc.scalar.activation(xnt[:, c % 2, eh, :], bank(e), ACT.Copy), e)
                elif e[0] == "v":
                    _, c, pair = e
                    t0 = (c % CPB) * CT + 2 * pair
                    wait_filled(act, e)
                    if (c, pair) == (0, 0):
                        act.wait_ge(consts_set, 1)
                    drained(nc.scalar.activation(v_sb[:, c // CPB, t0:t0 + 2, :, 0:HEAD_DIM],
                                                 bank(e).rearrange("p (t h d) -> p t h d", t=2, h=HEADS),
                                                 ACT.Copy), e)
                elif e[0] == "part1":
                    n = split_count[e[1:]]
                    act.wait_ge(rotated_ready, n)
                    if n > 2:
                        act.wait_ge(parts_stored[n % 2], 16 * PARTS * ((n - 1) // 2))
                    nc.scalar.activation(parts[:, n % 2, 0, :, :], rotated[:, :, :], ACT.Copy)\
                        .then_inc(part1_ready, 1)
                elif e[0] == "part2":
                    n = split_count[e[1:]]
                    act.wait_ge(rest_ready, n)
                    nc.scalar.activation(parts[:, n % 2, 1, :, :], rest[:, :, :], ACT.Copy).then_inc(part2_ready, 1)
                elif e[0] == "shift":
                    wait_filled(act, e)
                    if e[1]:
                        act.wait_ge(shift_placed, 32 * e[1])
                    n = 2 * HG * SEQ_TILES
                    drained(nc.scalar.activation(shift_t[:, :], bank(e)[0:n, 0:P // 2].bitcast(BF16), ACT.Copy), e)
                elif e[0] == "t":
                    _, g, q, h = e
                    n = quads[g, q]
                    wait_filled(act, e)
                    if h == 0 and n >= PR:
                        act.wait_ge(pv_done, n - PR + 1)
                    drained(nc.scalar.activation(probs[:, n % PR, h, :], bank(e), ACT.Exp, scale=SCALE), e)
                elif e[0] == "oev":
                    _, g, half = e
                    key = ("o", g, half)
                    act.wait_ge(pv_done, pv_count[g, HALF_LAST[half]])
                    drained(nc.scalar.activation(o_sb[:, half, :], bank(key), ACT.Copy), key)
                elif e[0] in ("xdt", "wt"):
                    wait_filled(act, e)
                    if e[0] == "wt":
                        drained(nc.scalar.activation(wt[:, :, :], bank(e).rearrange("p (a n) -> p a n", a=EH),
                                                     ACT.Copy), e)
                    else:
                        c, k = e[1:]
                        if k == 0 and c > 0:
                            key = ("ffn", c - 1, 1)
                            act.wait_ge(bank_filled[filling[key][0]], filling[key][1] + 1)
                        drained(nc.scalar.activation(xdt[:, k, :], bank(e), ACT.Copy), e)

        @block.vector
        def _(dve):
            chain = [0]

            def link(ins):
                chain[0] += 1
                ins.then_inc(dve_chain, 1)
                dve.wait_ge(dve_chain, chain[0])

            nc.vector.memset(block_max[:, :, :, :, :], LOWEST)
            for b in BANKS_O:
                ins = nc.vector.memset(ps[:, b, :], 0.0)
            ins.then_inc(psum_cleared, 1)
            for e in order:
                if e[0] == "ln":
                    c = e[1]
                    cs = slice(c * CT, (c + 1) * CT)
                    dve.wait_ge(x_loaded[c], 16)
                    for t in range(CT):
                        ins = nc.vector.bn_stats(stats[:, t, :], xs[:, c * CT + t, :])
                    link(ins)
                    for t in range(CT):
                        ins = nc.vector.bn_aggr(moments[:, c * CT + t, :], stats[:, t, :])
                    link(ins)
                    ins = nc.vector.tensor_scalar_add(variance[:, cs], moments[:, cs, 1], LN_EPS)
                    ins.then_inc(var_ready, 1)
                    dve.wait_ge(dev_ready, chunk_count[c])
                    link(nc.vector.reciprocal(rstd[:, cs], deviation[:, cs]))
                    link(nc.vector.tensor_tensor(newton[:, cs], rstd[:, cs], rstd[:, cs], ALU.mult))
                    link(nc.vector.tensor_tensor(newton[:, cs], newton[:, cs], variance[:, cs], ALU.mult))
                    link(nc.vector.tensor_scalar(newton[:, cs], newton[:, cs], -0.5, 1.5, ALU.mult, ALU.add))
                    link(nc.vector.tensor_tensor(rstd[:, cs], rstd[:, cs], newton[:, cs], ALU.mult))
                    for t in range(c * CT, (c + 1) * CT):
                        ins = nc.vector.tensor_scalar(xn[:, t, :], xs[:, t, :], moments[:, t, 0:1], rstd[:, t:t + 1],
                                                      ALU.subtract, ALU.mult)
                    ins.then_inc(xn_ready, 1)
                elif e[0] == "ckv":
                    wait_filled(dve, e)
                    if e[1] >= 2:
                        wait_filled(dve, ("proj", 1, e[1] - 2, 1))
                        wait_filled(dve, ("v", e[1] - 2, 1))
                    drained(nc.vector.tensor_copy(ckvt[:, e[1] % 2, :], bank(e)[0:LATENT, :]), e)
                elif e[0] == "proj":
                    _, t, c = e
                    n = split_count[t, c]
                    c0 = (c % CPB) * CHUNK
                    if n == 1:
                        dve.wait_ge(tables_loaded, 16 * 2 * HALF)
                    else:
                        dve.wait_ge(rotated_ready, n - 1)
                    for ab in range(2):
                        key = e + (ab,)
                        wait_filled(dve, key)
                        nc.vector.tensor_tensor(rope_products[:, 2 * ab, :], bank(key), cos_sb[:, c0:c0 + CHUNK],
                                                ALU.mult)
                        ins = nc.vector.tensor_tensor(rope_products[:, 2 * ab + 1, :], bank(key),
                                                      sin_sb[:, c0:c0 + CHUNK], ALU.mult)
                        drained(ins, key)
                elif e[0] == "rest1":
                    n = split_count[e[1:]]
                    dve.wait_ge(part1_ready, n)
                    if n > 1:
                        dve.wait_ge(part3_ready, n - 1)
                    nc.vector.tensor_tensor(rest[:, :, :], rotated[:, :, :], parts[:, n % 2, 0, :, :],
                                            ALU.subtract).then_inc(rest_ready, 1)
                elif e[0] == "s":
                    _, g, u = e
                    unit = UNITS[u]
                    h, i, j, n = unit[0]
                    wait_filled(dve, e)
                    to = block_max[:, g % 2, h:h + len(unit), i, j:j + n]
                    drained(nc.vector.tensor_reduce(
                        to, bank(e).rearrange("p (h j n) -> p h j n", h=len(unit), n=P), axis=AX.X, op=ALU.max), e)
                elif e[0] == "max":
                    g = e[1]
                    b, n = filling["s", g, len(UNITS) - 1]
                    dve.wait_ge(bank_drained[b], n + 1)
                    link(nc.vector.tensor_reduce(neg_max[:, :].rearrange("p (h i) -> p h i", h=HG),
                                                 block_max[:, g % 2, :, :, :], axis=AX.X, op=ALU.max, negate=True))
                    m = HG * SEQ_TILES
                    if g:
                        key = ("shift", g - 1)
                        dve.wait_ge(bank_filled[filling[key][0]], filling[key][1] + 1)
                    link(nc.vector.tensor_copy(shift_parts[:, 0:m], neg_max[:, :]))
                    nc.vector.tensor_tensor(shift_parts[:, m:2 * m], neg_max[:, :], shift_parts[:, 0:m],
                                            ALU.subtract).then_inc(shift_split, 1)
                elif e[0] == "ot":
                    _, g, half = e
                    wait_filled(dve, e)
                    if g:
                        dve.wait_ge(attn_added, ot_count[g - 1, half])
                    o = bank(e).rearrange("p (t h d) -> p t h d", t=CT, h=HG)
                    link(nc.vector.reciprocal(inv_sum[:, half, :, :], o[:, :, :, HEAD_DIM]))
                    ins = nc.vector.tensor_tensor(
                        attn[:, half, :, :, :], o[:, :, :, 0:HEAD_DIM],
                        inv_sum[:, half, :, :].unsqueeze(3).to_broadcast([P, CT, HG, HEAD_DIM]), ALU.mult)
                    drained(ins, e)
                elif e[0] == "scale":
                    c = e[1]
                    src, n = quant_source(c)
                    if c == "w":
                        dve.wait_ge(wffn_loaded, 16)
                    if quant_count[c] > 1:
                        dve.wait_ge(dequantized, quant_count[c] - 1)
                    link(nc.vector.tensor_reduce(amax[:, 0:n], src, axis=AX.X, op=ALU.max,
                                                 apply_absolute_value=True))
                    link(nc.vector.tensor_scalar(qscale[:, 0:n], amax[:, 0:n], 1.0 / FP8_MAX, None, ALU.mult))
                    nc.vector.reciprocal(qinv[:, 0:n], qscale[:, 0:n]).then_inc(scales_ready, 1)
                elif e[0] == "quant":
                    c = e[1]
                    _, n = quant_source(c)
                    dve.wait_ge(scaled_ready, quant_count[c])
                    nc.vector.tensor_scalar(qexp[:, 0:n, :].bitcast(U32), qx[:, 0:n, :].bitcast(U32), 0x7F800000,
                                            None, ALU.bitwise_and).then_inc(exponents_ready, 1)
                elif e[0] == "ffn":
                    _, c, pair = e
                    t0 = c * CT + 2 * pair
                    wait_filled(dve, e)
                    v = xs[:, t0:t0 + 2, :]
                    earlier = [k for k in ot_count if (k[0] // GPB, k[1]) == (c // CPB, c % CPB)
                               and at[("ot",) + k] < at[e]]
                    if earlier:
                        dve.wait_ge(attn_added, max(ot_count[k] for k in earlier))
                    ins = nc.vector.tensor_tensor(v, bank(e).rearrange("p (t n) -> p t n", t=2), v, ALU.add)
                    drained(ins, e)

        @block.tensor
        def _(pe):
            pe.wait_ge(consts_set, 1)
            pe.wait_ge(psum_cleared, 1)
            for e in order:
                if e[0] == "xt":
                    _, c, eh = e
                    pe.wait_ge(xn_ready, chunk_count[c])
                    wait_free(pe, e)
                    for t in range(CT):
                        ins = nc.tensor.transpose(bank(e)[:, t * P:(t + 1) * P],
                                                  xn[:, c * CT + t, eh * P:(eh + 1) * P], ident[:, :])
                    filled(ins, e)
                elif e[0] == "ckv":
                    c = e[1]
                    for eh in range(EH):
                        wait_drained(pe, ("xt", c, eh))
                    if c == 0:
                        pe.wait_ge(w_loaded, 64)
                    wait_free(pe, e)
                    for eh in range(EH):
                        ins = nc.tensor.matmul(bank(e)[0:LATENT, :], wkd_sb[:, eh, :], xnt[:, c % 2, eh, :],
                                               start=(eh == 0), stop=(eh == EH - 1))
                    filled(ins, e)
                elif e[0] == "proj":
                    _, t, c = e
                    for ab in range(2):
                        key = e + (ab,)
                        wait_free(pe, key)
                        if t == 0:
                            for eh in range(EH):
                                ins = nc.tensor.matmul(bank(key), wq_sb[:, eh, ab * P:(ab + 1) * P],
                                                       xnt[:, c % 2, eh, :], start=(eh == 0), stop=(eh == EH - 1))
                        else:
                            wait_drained(pe, ("ckv", c))
                            ins = nc.tensor.matmul(bank(key), wku_sb[:, ab * P:(ab + 1) * P], ckvt[:, c % 2, :],
                                                   start=True, stop=True)
                        filled(ins, key)
                elif e[0] == "v":
                    _, c, pair = e
                    wait_drained(pe, ("ckv", c))
                    wait_free(pe, e)
                    for t in range(2):
                        tok = (2 * pair + t) * P
                        ins = nc.tensor.matmul(bank(e)[:, t * EMBED:(t + 1) * EMBED], ckvt[:, c % 2, tok:tok + P],
                                               wv_sb[:, :], start=True, stop=True)
                    filled(ins, e)
                elif e[0] == "s":
                    _, g, u = e
                    if u == 0:
                        pe.wait_ge(kq_loaded[g % KQ_SLOTS], 16 * 12 * (g // KQ_SLOTS + 1))
                    wait_free(pe, e)
                    unit, k = UNITS[u], g % KQ_SLOTS
                    first, col = True, 0
                    for h, i, j, n in unit:
                        if j <= i < j + n and not (n == 1 and col):
                            at0 = col + (i - j) * P
                            w = 4 * P if n == 1 else P
                            nc.tensor.matmul(bank(e)[:, at0:at0 + w], ident_bf[:, :],
                                             mask_bf[:, 0:w // P, :].rearrange("p a n -> p (a n)"),
                                             start=first, stop=False, skip_group_check=True)
                            first = False
                        col += n * P
                    col = 0
                    for h, i, j, n in unit:
                        ins = nc.tensor.matmul(bank(e)[:, col:col + n * P], qt[0:SPLIT_ROWS, k, h, i * P:(i + 1) * P],
                                               kt[0:SPLIT_ROWS, k, h, j * P:(j + n) * P], start=first, stop=True,
                                               skip_group_check=True)
                        first = False
                        col += n * P
                    filled(ins, e)
                elif e[0] == "shift":
                    pe.wait_ge(shift_split, e[1] + 1)
                    wait_free(pe, e)
                    n = 2 * HG * SEQ_TILES
                    filled(nc.tensor.transpose(bank(e)[0:n, 0:P // 2].bitcast(BF16), shift_parts[:, :],
                                               ident_bf[:, :]), e)
                elif e[0] == "t":
                    _, g, q, h = e
                    if q == 0 and h == 0:
                        pe.wait_ge(shift_placed, 32 * (g + 1))
                    wait_free(pe, e)
                    k, col = g % KQ_SLOTS, 0
                    for _, j, q0, n in QUADS[q]:
                        ins = nc.tensor.matmul(bank(e)[:, col:col + n * P], kt[:, k, h, j * P:(j + 1) * P],
                                               qt[:, k, h, q0 * P:(q0 + n) * P], start=True, stop=True)
                        col += n * P
                    filled(ins, e)
                elif e[0] == "pv":
                    _, g, q = e
                    b = g // GPB
                    n = quads[g, q]
                    wait_drained(pe, ("t", g, q, HG - 1))
                    if DIAGONALS[q]:
                        pe.wait_ge(probs_zeroed, diag_count[g, q])
                    for half in range(2):
                        if q == HALF_FIRST[half]:
                            wait_free(pe, ("o", g, half))
                    col = 0
                    for s, (half, j, q0, w) in enumerate(QUADS[q]):
                        c0 = (q0 - half * CT) * P
                        for h in range(HG):
                            ins = nc.tensor.matmul(
                                ps[32 * h:32 * h + 17, BANKS_O[half], c0:c0 + w * P],
                                v_sb[:, b, j, (g % GPB) * HG + h, :],
                                probs[:, n % PR, h, col:col + w * P],
                                start=(q == HALF_FIRST[half]), stop=(q == HALF_LAST[half]), skip_group_check=True)
                        col += w * P
                        if s == len(QUADS[q]) - 1:
                            ins.then_inc(pv_done, 1)
                elif e[0] == "ot":
                    _, g, half = e
                    wait_drained(pe, ("o", g, half))
                    wait_free(pe, e)
                    for t in range(CT):
                        ins = nc.tensor.transpose(bank(e)[:, t * P:(t + 1) * P], o_sb[:, half, t * P:(t + 1) * P],
                                                  ident[:, :])
                    filled(ins, e)
                elif e[0] == "xdt":
                    _, c, k = e
                    pe.wait_ge(dequantized, quant_count[c])
                    wait_free(pe, e)
                    for t in range(CT):
                        ins = nc.tensor.transpose(bank(e)[:, t * P:(t + 1) * P], qx[:, 2 * t + k, :], ident[:, :])
                    filled(ins, e)
                elif e[0] == "wt":
                    pe.wait_ge(dequantized, quant_count["w"])
                    wait_free(pe, e)
                    for k in range(EH):
                        for a in range(EH):
                            ins = nc.tensor.transpose(bank(e)[:, (k * EH + a) * P:(k * EH + a + 1) * P],
                                                      qx[:, a * EH + k, :], ident[:, :])
                    filled(ins, e)
                elif e[0] == "ffn":
                    _, c, pair = e
                    for k in range(EH):
                        wait_drained(pe, ("xdt", c, k))
                    wait_drained(pe, ("wt",))
                    wait_free(pe, e)
                    for t in range(2):
                        tok = (2 * pair + t) * P
                        for k in range(EH):
                            ins = nc.tensor.matmul(bank(e)[:, t * EMBED:(t + 1) * EMBED], xdt[:, k, tok:tok + P],
                                                   wt[:, k, :], start=(k == 0), stop=(k == EH - 1))
                    filled(ins, e)


def rope_tables():
    import numpy as np
    freqs = np.float32(1.0) / np.power(np.float32(THETA), np.arange(0, ROPE, 2, dtype=np.float32) / np.float32(ROPE))
    angle = freqs.astype(np.float32)[:, None] * np.arange(SEQ, dtype=np.float32)[None, :]
    still = np.zeros((NOPE // 2, SEQ), np.float32)
    angle = np.concatenate([still, angle]).astype(np.float32)
    return np.cos(angle).astype(np.float32), np.sin(angle).astype(np.float32)


def column_order():
    first = list(range(NOPE // 2)) + list(range(NOPE, HEAD_DIM, 2))
    second = list(range(NOPE // 2, NOPE)) + list(range(NOPE + 1, HEAD_DIM, 2))
    return [h * HEAD_DIM + d for dims in (first, second) for d in dims for h in range(HEADS)]


def kernel(**inputs):
    import numpy as np
    import concourse.bacc as bacc
    from concourse.bass_utils import run_bass_kernel_spmd

    cos, sin = rope_tables()
    cols = column_order()
    arrays = {
        "x": np.ascontiguousarray(inputs["L0_attn_x"]),
        "wq": np.ascontiguousarray(np.asarray(inputs["L0_attn_Wq"])[:, cols]),
        "wkd": np.ascontiguousarray(inputs["L0_attn_Wkv_down"]),
        "wku": np.ascontiguousarray(np.asarray(inputs["L0_attn_Wk_up"])[:, cols]),
        "wv": np.ascontiguousarray(inputs["L0_attn_Wv_up"]),
        "wffn": np.ascontiguousarray(inputs["L0_ffn_weight"]),
        "cos": cos,
        "sin": sin,
    }
    nc = bacc.Bacc("TRN2", target_bir_lowering=False, num_devices=1)
    aps = {n: nc.dram_tensor(n, a.shape, mybir.dt.from_np(a.dtype), kind="ExternalInput").ap()
           for n, a in arrays.items()}
    out = nc.dram_tensor("out", (BATCH, SEQ, EMBED), F32, kind="ExternalOutput").ap()
    build(nc, *aps.values(), out)
    r = run_bass_kernel_spmd(nc, [arrays], core_ids=[0])
    return r.results[0]["out"]
```

```python
from contextlib import ExitStack

import concourse.bass as bass
from concourse import mybir

ALU = mybir.AluOpType
ACT = mybir.ActivationFunctionType
AX = mybir.AxisListType
F32 = mybir.dt.float32
BF16 = mybir.dt.bfloat16
U32 = mybir.dt.uint32

P = 128
BATCH, SEQ, EMBED = 2, 1024, 256
HEADS, LATENT = 16, 64
HEAD_DIM = EMBED // HEADS
NOPE = HEAD_DIM // 4
ROPE = HEAD_DIM - NOPE
SCALE = HEAD_DIM ** -0.5
LN_EPS = 1e-5
THETA = 10000.0

TILES = BATCH * SEQ // P
SEQ_TILES = SEQ // P
CHUNK = 512
CT = CHUNK // P
CHUNKS = BATCH * SEQ // CHUNK
CPB = SEQ // CHUNK
HG = 4
GROUPS = BATCH * HEADS // HG
GPB = HEADS // HG
HALF = HEAD_DIM // 2
EH = EMBED // P

PARTS = 3
Q_SLOTS = [0, 0, 0, 1, 1, 2]
K_SLOTS = [0, 1, 2, 0, 1, 0]
SPLIT_ROWS = len(Q_SLOTS) * HEAD_DIM
ALL_ROWS = SPLIT_ROWS + 2
VC = 32

QBLOCK = 128
FP8_MAX = 448.0
FP8_LEAST_NORMAL = 2.0 ** -6
ROUND_3_BITS = 1.5 * 2.0 ** 20
MASKED = -1e30
LOWEST = -3e38
TWO_BF16_ONES = 1.0 + 0x3F80 / 2.0 ** 23

NS, NT, NA = 2, 2, 2
BANKS_S = list(range(NS))
BANKS_T = list(range(NS, NS + NT))
BANKS_O = [NS + NT, NS + NT + 1]
BANKS_A = list(range(NS + NT + 2, NS + NT + 2 + NA))
KQ_SLOTS = 3
PR = 3
LOADS = 6
LEAD = 2


def max_units():
    units = [[(h, i, j, 4)] for i, j in ((3, 0), (7, 0), (7, 4), (4, 0), (5, 0), (6, 0)) for h in range(HG)]
    units += [[(h, i, j, 2) for h in (hp, hp + 1)] for i, j in ((1, 0), (2, 0), (5, 4), (6, 4)) for hp in (0, 2)]
    units += [[(h, i, j, 1) for h in range(HG)] for i, j in ((0, 0), (4, 4), (2, 2), (6, 6))]
    return units


QUADS = [
    [(0, 0, 0, 4)],
    [(0, 1, 1, 3), (0, 3, 3, 1)],
    [(1, 0, 4, 4)],
    [(0, 2, 2, 2), (1, 6, 6, 2)],
    [(1, 1, 4, 4)],
    [(1, 2, 4, 4)],
    [(1, 3, 4, 4)],
    [(1, 4, 4, 4)],
    [(1, 5, 5, 3), (1, 7, 7, 1)],
]
UNITS = max_units()
NQ = len(QUADS)
HALF_FIRST = [0, 2]
HALF_LAST = [3, 8]


def diagonals(q):
    out, col = [], 0
    for _, j, q0, n in QUADS[q]:
        if q0 == j:
            out.append(col)
        col += n * P
    return out


DIAGONALS = [diagonals(q) for q in range(NQ)]


def plan():
    order = [("stats", 0), ("root", 0), ("norm", 0), ("stats", 1), ("root", 1), ("xt", 0, 0), ("xt", 0, 1),
             ("norm", 1), ("ckv", 0), ("xt", 1, 0), ("xt", 1, 1), ("proj", 0, 0, 0), ("proj", 0, 0, 1),
             ("rope", 0, 0), ("proj", 1, 0, 0), ("proj", 1, 0, 1), ("part1", 0, 0), ("rope", 1, 0), ("ckv", 1),
             ("rest", 0, 0), ("part1", 1, 0), ("part2", 0, 0), ("proj", 0, 1, 0), ("rest", 1, 0), ("proj", 0, 1, 1),
             ("part3", 0, 0), ("part2", 1, 0), ("rope", 0, 1), ("proj", 1, 1, 0), ("part1", 0, 1), ("proj", 1, 1, 1),
             ("part3", 1, 0), ("rope", 1, 1), ("rest", 0, 1), ("part1", 1, 1), ("part2", 0, 1), ("v", 0, 0),
             ("rest", 1, 1), ("part3", 0, 1), ("part2", 1, 1), ("part3", 1, 1)]
    order += [("load", 0, n) for n in range(LOADS)]
    order += [(k, c) for c in range(CPB, CHUNKS) for k in ("stats", "root", "norm")]
    order += [("v", 0, 1), ("v", 1, 0), ("v", 1, 1)]
    order += [("load", g, n) for g in (1, 2) for n in range(LOADS)]

    jobs = []
    for n, c in enumerate(range(CPB, CHUNKS)):
        jobs.append((8 * n, [
            [("xt", c, 0)], [("xt", c, 1)], [("ckv", c)], [("proj", 0, c, 0)], [("proj", 0, c, 1)],
            [("rope", 0, c), ("proj", 1, c, 0)], [("part1", 0, c), ("proj", 1, c, 1)],
            [("rest", 0, c), ("rope", 1, c)], [("part2", 0, c), ("v", c, 0)], [("part3", 0, c), ("part1", 1, c)],
            [("v", c, 1), ("rest", 1, c)], [("part2", 1, c)], [("part3", 1, c)]]))
    for n, c in enumerate(["w"] + list(range(CHUNKS))):
        jobs.append((20 + 6 * n, [[("scale", c)], [("quant", c)], [("expo", c)], [("round", c)], [("dequant", c)], []] + (
            [[("wt",)]] if c == "w" else [[("xdt", c, 0), ("xdt", c, 1)], [("ffn", c, 0)], [("ffn", c, 1)]])))
    side = [[e for start, pieces in jobs if start <= n < start + len(pieces) for e in pieces[n - start]]
            for n in range(max(start + len(pieces) for start, pieces in jobs))]

    maxima = [(g, u) for g in range(GROUPS) for u in range(len(UNITS))]
    for n in range(len(UNITS) + LEAD * HG):
        order.append(("s",) + maxima.pop(0))
        if n % 5 == 4:
            order += side.pop(0)
        if n == len(UNITS) - 1:
            order.append(("max", 0))
        if n == len(UNITS) + 1:
            order.append(("shift", 0))

    steps = [(g, q) for g in range(GROUPS) for q in range(NQ)]
    for n, (g, q) in enumerate(steps):
        for h in range(HG):
            if maxima:
                order.append(("s",) + maxima.pop(0))
            order.append(("t", g, q, h))
            if h == 1 and n >= 2:
                order.append(("pv",) + steps[n - 2])
                if steps[n - 2][1] in HALF_LAST:
                    order.append(("oev", steps[n - 2][0], HALF_LAST.index(steps[n - 2][1])))
        if DIAGONALS[q]:
            order.append(("diag", g, q))
        if q < LOADS and KQ_SLOTS <= g - 1 + KQ_SLOTS < GROUPS and g - 1 + KQ_SLOTS != GPB:
            order.append(("load", g - 1 + KQ_SLOTS, q))
        if q == NQ - LEAD - 1 and g + 1 < GROUPS:
            order.append(("max", g + 1))
        if q == NQ - LEAD and g + 1 < GROUPS:
            order.append(("shift", g + 1))
        if n >= 3 and steps[n - 3][1] in HALF_LAST:
            order.append(("ot", steps[n - 3][0], HALF_LAST.index(steps[n - 3][1])))
        elif side:
            order += side[0]
            if ("part3", 1, CHUNKS - 1) in side.pop(0):
                order += [("load", GPB, n) for n in range(LOADS)]
    assert not side and not maxima
    g = GROUPS - 1
    order += [("pv", g, NQ - 2), ("pv", g, NQ - 1), ("oev", g, 1), ("ot", g, 1)]
    for c in range(CHUNKS):
        last = [("ot", (c // CPB + 1) * GPB - 1, c % CPB), ("ffn", c, 0), ("ffn", c, 1)]
        order.insert(max(order.index(e) for e in last) + 1, ("out", c))
    return order


def build(nc, x, wq, wkd, wku, wv, wffn, cos, sin, out):
    order = plan()
    at = {e: n for n, e in enumerate(order)}
    assert len(at) == len(order)

    filling, fillings, turn = {}, [0] * 8, {"s": 0, "t": 0, "a": 0}

    def take(key, kind, banks):
        b = banks[turn[kind] % len(banks)]
        turn[kind] += 1
        filling[key] = (b, fillings[b])
        fillings[b] += 1

    for e in order:
        if e[0] == "s":
            take(e, "s", BANKS_S)
        elif e[0] == "t":
            take(e, "t", BANKS_T)
        elif e[0] == "pv":
            for half in range(2):
                if e[2] == HALF_LAST[half]:
                    b = BANKS_O[half]
                    filling["o", e[1], half] = (b, fillings[b])
                    fillings[b] += 1
        elif e[0] in ("proj", "xt", "ckv", "v", "shift", "ot", "xdt", "ffn", "wt"):
            take(e, "a", BANKS_A)
    ring = {e: n for n, e in enumerate(e for e in order if e[0] == "t")}
    quads = {e[1:3]: n // HG for e, n in ring.items()}
    diag_count = {e[1:]: n + 1 for n, e in enumerate(e for e in order if e[0] == "diag")}
    pv_count = {e[1:]: n + 1 for n, e in enumerate(e for e in order if e[0] == "pv")}
    ot_count = {e[1:]: n + 1 for n, e in enumerate(e for e in order if e[0] == "ot")}
    split_count = {e[1:3]: n + 1 for n, e in enumerate(e for e in order if e[0] == "proj" and e[3] == 0)}
    chunk_count = {e[1]: n + 1 for n, e in enumerate(e for e in order if e[0] == "stats")}
    quant_count = {e[1]: n + 1 for n, e in enumerate(e for e in order if e[0] == "scale")}
    ffn_count = {e[1:]: n + 1 for n, e in enumerate(e for e in order if e[0] == "ffn")}
    xdt_count = {e[1:]: n + 1 for n, e in enumerate(e for e in order if e[0] == "xdt")}

    with ExitStack() as ctx:
        def sb(name, shape, dt=F32):
            return ctx.enter_context(nc.sbuf_tensor(name, shape, dt))

        def sem(name):
            return ctx.enter_context(nc.semaphore(name))

        xs = sb("xs", [P, TILES, EMBED])
        wq_sb = sb("wq_sb", [P, EH, EMBED])
        wkd_sb = sb("wkd_sb", [P, EH, LATENT])
        wku_sb = sb("wku_sb", [LATENT, EMBED])
        wv_sb = sb("wv_sb", [LATENT, EMBED])
        w_sb = sb("w_sb", [P, EH, EMBED])
        cos_sb = sb("cos_sb", [P, SEQ])
        sin_sb = sb("sin_sb", [P, SEQ])
        ident = sb("ident", [P, P])
        ident_bf = sb("ident_bf", [P, P], BF16)
        mask_bf = sb("mask_bf", [P, 4, P], BF16)
        stats = sb("stats", [P, CT, 6])
        moments = sb("moments", [P, TILES, 2])
        variance = sb("variance", [P, TILES])
        deviation = sb("deviation", [P, TILES])
        rstd = sb("rstd", [P, TILES])
        newton = sb("newton", [P, TILES])
        xn = sb("xn", [P, TILES, EMBED])
        xnt = sb("xnt", [P, 2, EH, CHUNK])
        ckvt = sb("ckvt", [LATENT, 2, CHUNK])
        rope_products = sb("rope_products", [P, 2, 4, CHUNK])
        rotated = sb("rotated", [P, 2, 2, CHUNK])
        rest = sb("rest", [P, 2, 2, CHUNK])
        parts = sb("parts", [P, 2, PARTS, 2, CHUNK], BF16)
        v_sb = sb("v_sb", [P, BATCH, SEQ_TILES, HEADS, 17])
        qt = sb("qt", [ALL_ROWS, KQ_SLOTS, HG, SEQ], BF16)
        kt = sb("kt", [ALL_ROWS, KQ_SLOTS, HG, SEQ], BF16)
        block_max = sb("block_max", [P, 2, HG, SEQ_TILES, SEQ_TILES])
        neg_max = sb("neg_max", [P, HG * SEQ_TILES])
        shift_parts = sb("shift_parts", [P, 2 * HG * SEQ_TILES], BF16)
        shift_t = sb("shift_t", [2 * HG * SEQ_TILES, P], BF16)
        probs = sb("probs", [P, PR, HG, CHUNK])
        o_sb = sb("o_sb", [P, 2, CHUNK])
        inv_sum = sb("inv_sum", [P, 2, CT, HG])
        attn = sb("attn", [P, 2, CT, HG, HEAD_DIM])
        amax = sb("amax", [P, 8])
        qscale = sb("qscale", [P, 8])
        qinv = sb("qinv", [P, 8])
        qexp = sb("qexp", [P, 8, QBLOCK])
        wt = wq_sb

        ps = ctx.enter_context(nc.psum_tensor("ps", [P, 8, 512], F32))
        scratch = nc.dram_tensor("split_scratch", [2, BATCH, PARTS, 2, P, SEQ], BF16).ap()

        bank_filled = [sem(f"bank_filled{b}") for b in range(8)]
        bank_drained = [sem(f"bank_drained{b}") for b in range(8)]
        x_loaded = [sem(f"x_loaded{c}") for c in range(CHUNKS)]
        w_loaded = sem("w_loaded")
        wffn_loaded = sem("wffn_loaded")
        tables_loaded = sem("tables_loaded")
        consts_set = sem("consts_set")
        psum_cleared = sem("psum_cleared")
        dve_chain = sem("dve_chain")
        pool_chain = sem("pool_chain")
        var_ready = sem("var_ready")
        dev_ready = sem("dev_ready")
        xn_ready = sem("xn_ready")
        rotated_ready = sem("rotated_ready")
        part1_ready = sem("part1_ready")
        rest_ready = sem("rest_ready")
        part2_ready = sem("part2_ready")
        part3_ready = sem("part3_ready")
        parts_stored = [sem(f"parts_stored{k}") for k in range(2)]
        kq_loaded = [sem(f"kq_loaded{k}") for k in range(KQ_SLOTS)]
        shift_split = sem("shift_split")
        shift_placed = sem("shift_placed")
        probs_zeroed = sem("probs_zeroed")
        pv_done = sem("pv_done")
        attn_added = sem("attn_added")
        scales_ready = sem("scales_ready")
        scaled_ready = sem("scaled_ready")
        exponents_ready = sem("exponents_ready")
        rounded = sem("rounded")
        dequantized = sem("dequantized")
        out_stored = sem("out_stored")

        def bank(key):
            return ps[:, filling[key][0], :]

        def wait_filled(eng, key):
            b, n = filling[key]
            eng.wait_ge(bank_filled[b], n + 1)

        def wait_free(eng, key):
            b, n = filling[key]
            if n:
                eng.wait_ge(bank_drained[b], n)

        def wait_drained(eng, key):
            b, n = filling[key]
            eng.wait_ge(bank_drained[b], n + 1)

        def filled(ins, key):
            ins.then_inc(bank_filled[filling[key][0]], 1)

        def drained(ins, key):
            ins.then_inc(bank_drained[filling[key][0]], 1)

        def quant_blocks(c):
            if c == "w":
                return w_sb[:, :, :].rearrange("p a (k f) -> p (a k) f", f=QBLOCK), EH * EMBED // QBLOCK
            return (xn[:, c * CT:(c + 1) * CT, :].rearrange("p a (k f) -> p (a k) f", f=QBLOCK),
                    CT * EMBED // QBLOCK)

        def rotate(eng, unit, e):
            n = split_count[e[1:]]
            products, to = rope_products[:, n % 2, :, :], rotated[:, n % 2, :, :]
            wait_drained(eng, ("proj",) + e[1:] + (1,))
            if n > 2:
                eng.wait_ge(rest_ready, n - 2)
            unit.tensor_tensor(to[:, 0, :], products[:, 0, :], products[:, 3, :], ALU.subtract)
            unit.tensor_tensor(to[:, 1, :], products[:, 2, :], products[:, 1, :], ALU.add).then_inc(rotated_ready, 1)

        block = ctx.enter_context(nc.Block())

        @block.sync
        def _(sp):
            xv = x.rearrange("b (t p) e -> p (b t) e", p=P)
            def load_x(c):
                sp.dma_start(xs[:, c * CT:(c + 1) * CT, :], xv[:, c * CT:(c + 1) * CT, :]).then_inc(x_loaded[c], 16)

            load_x(0)
            sp.dma_start(wkd_sb[:, :, :], wkd.rearrange("(a p) n -> p a n", p=P)).then_inc(w_loaded, 16)
            load_x(1)
            sp.dma_start(wq_sb[:, :, :], wq.rearrange("(a p) n -> p a n", p=P)).then_inc(w_loaded, 16)
            sp.dma_start(wku_sb[:, :], wku).then_inc(w_loaded, 16)
            sp.dma_start(wv_sb[:, :], wv).then_inc(w_loaded, 16)
            for dst, src in ((cos_sb, cos), (sin_sb, sin)):
                rows = bass.AP(src.tensor, src.offset, [[SEQ, HALF], [0, HEADS], [1, SEQ]])
                sp.dma_start(dst[:, :], rows).then_inc(tables_loaded, 16)
            for c in range(2, CHUNKS):
                load_x(c)
            sp.dma_start(w_sb[:, :, :], wffn.rearrange("(a p) n -> p a n", p=P)).then_inc(wffn_loaded, 16)
            outs = 0
            for e in order:
                if e[0] in ("part1", "part2", "part3"):
                    _, t, c = e
                    n, part = split_count[t, c], int(e[0][-1]) - 1
                    b, c0 = c // CPB, (c % CPB) * CHUNK
                    sp.wait_ge((part1_ready, part2_ready, part3_ready)[part], n)
                    sp.dma_start(scratch[t, b, part, :, :, c0:c0 + CHUNK].rearrange("a p n -> p a n"),
                                 parts[:, n % 2, part, :, :]).then_inc(parts_stored[n % 2], 16)
                elif e[0] == "load":
                    _, g, portion = e
                    b, h0 = g // GPB, (g % GPB) * HG
                    if portion == 0:
                        for k in range(2):
                            sp.wait_ge(parts_stored[k], 16 * PARTS * CPB * (b + 1))
                        if g >= KQ_SLOTS:
                            wait_filled(sp, ("t", g - KQ_SLOTS, NQ - 1, HG - 1))
                    for t, (dst, slots) in enumerate(((qt, Q_SLOTS), (kt, K_SLOTS))):
                        rows = scratch[t, b].rearrange("s a (d h) n -> (s a d) (h n)", h=HEADS)
                        part = slots[portion]
                        sp.dma_start(dst[portion * HEAD_DIM:(portion + 1) * HEAD_DIM, g % KQ_SLOTS, :, :]
                                     .rearrange("p h n -> p (h n)"),
                                     rows[part * HEAD_DIM:(part + 1) * HEAD_DIM, h0 * SEQ:(h0 + HG) * SEQ])\
                          .then_inc(kq_loaded[g % KQ_SLOTS], 16)
                elif e[0] == "out":
                    c = e[1]
                    sp.wait_ge(attn_added, ot_count[(c // CPB + 1) * GPB - 1, c % CPB])
                    for pair in range(2):
                        wait_drained(sp, ("ffn", c, pair))
                    sp.dma_start(out.rearrange("b (t p) e -> p (b t) e", p=P)[:, c * CT:(c + 1) * CT, :],
                                 xs[:, c * CT:(c + 1) * CT, :]).then_inc(out_stored, 16)
                    outs += 16
            sp.wait_ge(out_stored, outs)

        @block.gpsimd
        def _(pool):
            chain = [0]

            def link(ins):
                chain[0] += 1
                ins.then_inc(pool_chain, 1)
                pool.wait_ge(pool_chain, chain[0])

            nc.gpsimd.memset(ident[:, :], 0.0)
            nc.gpsimd.memset(ident_bf[:, :], 0.0)
            nc.gpsimd.memset(mask_bf[:, :, :], 0.0)
            link(nc.gpsimd.memset(v_sb[:, :, :, :, HEAD_DIM:17], 1.0))
            link(nc.gpsimd.memset(kt[SPLIT_ROWS:ALL_ROWS, :, :, :].rearrange("p a b n -> p (a b n)").bitcast(F32),
                                  TWO_BF16_ONES))
            for m in (ident, ident_bf):
                nc.gpsimd.affine_select(out=m[:, :], in_=m[:, :], compare_op=ALU.not_equal, fill=1.0,
                                        base=0, pattern=[[-1, P]], channel_multiplier=1)
            nc.gpsimd.affine_select(out=mask_bf[:, :, :], in_=mask_bf[:, :, :], compare_op=ALU.is_ge, fill=MASKED,
                                    base=0, pattern=[[0, 4], [-1, P]], channel_multiplier=1).then_inc(consts_set, 1)
            for e in order:
                if e[0] == "rope" and e[2] >= CPB:
                    rotate(pool, nc.gpsimd, e)
                elif e[0] == "part3":
                    n = split_count[e[1:]]
                    pool.wait_ge(part2_ready, n)
                    nc.gpsimd.tensor_tensor(parts[:, n % 2, 2, :, :], rest[:, n % 2, :, :], parts[:, n % 2, 1, :, :],
                                            ALU.subtract).then_inc(part3_ready, 1)
                elif e[0] == "diag":
                    _, g, q = e
                    wait_drained(pool, ("t", g, q, HG - 1))
                    for n, col in enumerate(DIAGONALS[q]):
                        v = probs[:, quads[g, q] % PR, :, col:col + P]
                        ins = nc.gpsimd.affine_select(out=v, in_=v, compare_op=ALU.is_ge, fill=0.0, base=0,
                                                      pattern=[[0, HG], [1, P]], channel_multiplier=-1)
                    ins.then_inc(probs_zeroed, 1)
                elif e[0] == "ot":
                    _, g, half = e
                    b, h0 = g // GPB, (g % GPB) * HG
                    t0 = b * SEQ_TILES + half * CT
                    wait_drained(pool, e)
                    for pair in range(2):
                        key = ("ffn", t0 // CT, pair)
                        if at[key] < at[e]:
                            wait_drained(pool, key)
                    dst = xs[:, t0:t0 + CT, h0 * HEAD_DIM:(h0 + HG) * HEAD_DIM]
                    src = attn[:, half, :, :, :].rearrange("p t h d -> p t (h d)")
                    nc.gpsimd.tensor_tensor(dst, dst, src, ALU.add).then_inc(attn_added, 1)
                elif e[0] == "quant":
                    c = e[1]
                    v, n = quant_blocks(c)
                    pool.wait_ge(scales_ready, quant_count[c])
                    nc.gpsimd.tensor_tensor(v, v,
                                            qinv[:, 0:n].unsqueeze(2).to_broadcast([P, n, QBLOCK]),
                                            ALU.mult).then_inc(scaled_ready, 1)
                elif e[0] == "round":
                    c = e[1]
                    v, n = quant_blocks(c)
                    pool.wait_ge(exponents_ready, quant_count[c])
                    link(nc.gpsimd.tensor_tensor(v, v, qexp[:, 0:n, :], ALU.add))
                    nc.gpsimd.tensor_tensor(v, v, qexp[:, 0:n, :], ALU.subtract).then_inc(rounded, 1)
                elif e[0] == "dequant":
                    c = e[1]
                    v, n = quant_blocks(c)
                    pool.wait_ge(rounded, quant_count[c])
                    nc.gpsimd.tensor_tensor(v, v, qscale[:, 0:n].unsqueeze(2).to_broadcast([P, n, QBLOCK]),
                                            ALU.mult).then_inc(dequantized, 1)

        @block.scalar
        def _(act):
            for e in order:
                if e[0] == "root":
                    c = e[1]
                    act.wait_ge(var_ready, chunk_count[c])
                    nc.scalar.activation(deviation[:, c * CT:(c + 1) * CT], variance[:, c * CT:(c + 1) * CT],
                                         ACT.Sqrt).then_inc(dev_ready, 1)
                elif e[0] == "xt":
                    _, c, eh = e
                    wait_filled(act, e)
                    if c >= 2:
                        wait_filled(act, ("proj", 0, c - 2, 1))
                    drained(nc.scalar.activation(xnt[:, c % 2, eh, :], bank(e), ACT.Copy), e)
                elif e[0] == "v":
                    _, c, pair = e
                    t0 = (c % CPB) * CT + 2 * pair
                    wait_filled(act, e)
                    if (c, pair) == (0, 0):
                        act.wait_ge(consts_set, 1)
                    drained(nc.scalar.activation(v_sb[:, c // CPB, t0:t0 + 2, :, 0:HEAD_DIM],
                                                 bank(e).rearrange("p (t h d) -> p t h d", t=2, h=HEADS),
                                                 ACT.Copy), e)
                elif e[0] == "part1":
                    n = split_count[e[1:]]
                    act.wait_ge(rotated_ready, n)
                    if n > 2:
                        act.wait_ge(parts_stored[n % 2], 16 * PARTS * ((n - 1) // 2))
                    nc.scalar.activation(parts[:, n % 2, 0, :, :], rotated[:, n % 2, :, :], ACT.Copy)\
                        .then_inc(part1_ready, 1)
                elif e[0] == "part2":
                    n = split_count[e[1:]]
                    act.wait_ge(rest_ready, n)
                    nc.scalar.activation(parts[:, n % 2, 1, :, :], rest[:, n % 2, :, :], ACT.Copy).then_inc(part2_ready, 1)
                elif e[0] == "shift":
                    wait_filled(act, e)
                    if e[1]:
                        act.wait_ge(shift_placed, 32 * e[1])
                    n = 2 * HG * SEQ_TILES
                    drained(nc.scalar.activation(shift_t[:, :], bank(e)[0:n, 0:P // 2].bitcast(BF16), ACT.Copy), e)
                    g, n = e[1], HG * SEQ_TILES
                    wait_drained(act, e)
                    for part in range(2):
                        row = SPLIT_ROWS + part
                        act.dma_start(qt[row:row + 1, g % KQ_SLOTS, :, :].rearrange("p h (i n) -> p (h i) n", n=P),
                                      shift_t[part * n:(part + 1) * n, :]).then_inc(shift_placed, 16)
                elif e[0] == "t":
                    _, g, q, h = e
                    n = quads[g, q]
                    wait_filled(act, e)
                    if h == 0 and n >= PR:
                        act.wait_ge(pv_done, n - PR + 1)
                    drained(nc.scalar.activation(probs[:, n % PR, h, :], bank(e), ACT.Exp, scale=SCALE), e)
                elif e[0] == "oev":
                    _, g, half = e
                    key = ("o", g, half)
                    act.wait_ge(pv_done, pv_count[g, HALF_LAST[half]])
                    drained(nc.scalar.activation(o_sb[:, half, :], bank(key), ACT.Copy), key)
                elif e[0] in ("xdt", "wt"):
                    wait_filled(act, e)
                    if e[0] == "wt":
                        wait_filled(act, ("proj", 0, CHUNKS - 1, 1))
                        drained(nc.scalar.activation(wt[:, :, :], bank(e).rearrange("p (a n) -> p a n", a=EH),
                                                     ACT.Copy), e)
                    else:
                        c, k = e[1:]
                        wait_filled(act, ("proj", 0, c + 2, 1) if c < 2 else ("ffn", c - 2, 1))
                        drained(nc.scalar.activation(xnt[:, c % 2, k, :], bank(e), ACT.Copy), e)

        @block.vector
        def _(dve):
            chain = [0]

            def link(ins):
                chain[0] += 1
                ins.then_inc(dve_chain, 1)
                dve.wait_ge(dve_chain, chain[0])

            nc.vector.memset(block_max[:, :, :, :, :], LOWEST)
            for b in BANKS_O:
                ins = nc.vector.memset(ps[:, b, :], 0.0)
            ins.then_inc(psum_cleared, 1)
            for e in order:
                if e[0] == "stats":
                    c = e[1]
                    cs = slice(c * CT, (c + 1) * CT)
                    dve.wait_ge(x_loaded[c], 16)
                    for t in range(CT):
                        ins = nc.vector.bn_stats(stats[:, t, :], xs[:, c * CT + t, :])
                    link(ins)
                    for t in range(CT):
                        ins = nc.vector.bn_aggr(moments[:, c * CT + t, :], stats[:, t, :])
                    link(ins)
                    ins = nc.vector.tensor_scalar_add(variance[:, cs], moments[:, cs, 1], LN_EPS)
                    ins.then_inc(var_ready, 1)
                elif e[0] == "norm":
                    c = e[1]
                    cs = slice(c * CT, (c + 1) * CT)
                    dve.wait_ge(dev_ready, chunk_count[c])
                    link(nc.vector.reciprocal(rstd[:, cs], deviation[:, cs]))
                    link(nc.vector.tensor_tensor(newton[:, cs], rstd[:, cs], rstd[:, cs], ALU.mult))
                    link(nc.vector.tensor_tensor(newton[:, cs], newton[:, cs], variance[:, cs], ALU.mult))
                    link(nc.vector.tensor_scalar(newton[:, cs], newton[:, cs], -0.5, 1.5, ALU.mult, ALU.add))
                    link(nc.vector.tensor_tensor(rstd[:, cs], rstd[:, cs], newton[:, cs], ALU.mult))
                    for t in range(c * CT, (c + 1) * CT):
                        ins = nc.vector.tensor_scalar(xn[:, t, :], xs[:, t, :], moments[:, t, 0:1], rstd[:, t:t + 1],
                                                      ALU.subtract, ALU.mult)
                    ins.then_inc(xn_ready, 1)
                elif e[0] == "ckv":
                    wait_filled(dve, e)
                    if e[1] >= 2:
                        wait_filled(dve, ("proj", 1, e[1] - 2, 1))
                        wait_filled(dve, ("v", e[1] - 2, 1))
                    drained(nc.vector.tensor_copy(ckvt[:, e[1] % 2, :], bank(e)[0:LATENT, :]), e)
                elif e[0] == "proj":
                    _, t, c, ab = e
                    n = split_count[t, c]
                    c0 = (c % CPB) * CHUNK
                    if n == 1:
                        dve.wait_ge(tables_loaded, 16 * 2)
                    if n > 2 and ab == 0:
                        dve.wait_ge(rotated_ready, n - 2)
                    wait_filled(dve, e)
                    nc.vector.tensor_tensor(rope_products[:, n % 2, 2 * ab, :], bank(e), cos_sb[:, c0:c0 + CHUNK],
                                            ALU.mult)
                    drained(nc.vector.tensor_tensor(rope_products[:, n % 2, 2 * ab + 1, :], bank(e),
                                                    sin_sb[:, c0:c0 + CHUNK], ALU.mult), e)
                elif e[0] == "rope" and e[2] < CPB:
                    rotate(dve, nc.vector, e)
                elif e[0] == "rest":
                    n = split_count[e[1:]]
                    dve.wait_ge(part1_ready, n)
                    if n > 2:
                        dve.wait_ge(part3_ready, n - 2)
                    nc.vector.tensor_tensor(rest[:, n % 2, :, :], rotated[:, n % 2, :, :], parts[:, n % 2, 0, :, :],
                                            ALU.subtract).then_inc(rest_ready, 1)
                elif e[0] == "s":
                    _, g, u = e
                    unit = UNITS[u]
                    h, i, j, n = unit[0]
                    wait_filled(dve, e)
                    to = block_max[:, g % 2, h:h + len(unit), i, j:j + n]
                    drained(nc.vector.tensor_reduce(
                        to, bank(e).rearrange("p (h j n) -> p h j n", h=len(unit), n=P), axis=AX.X, op=ALU.max), e)
                elif e[0] == "max":
                    g = e[1]
                    b, n = filling["s", g, len(UNITS) - 1]
                    dve.wait_ge(bank_drained[b], n + 1)
                    link(nc.vector.tensor_reduce(neg_max[:, :].rearrange("p (h i) -> p h i", h=HG),
                                                 block_max[:, g % 2, :, :, :], axis=AX.X, op=ALU.max, negate=True))
                    m = HG * SEQ_TILES
                    if g:
                        key = ("shift", g - 1)
                        dve.wait_ge(bank_filled[filling[key][0]], filling[key][1] + 1)
                    link(nc.vector.tensor_copy(shift_parts[:, 0:m], neg_max[:, :]))
                    nc.vector.tensor_tensor(shift_parts[:, m:2 * m], neg_max[:, :], shift_parts[:, 0:m],
                                            ALU.subtract).then_inc(shift_split, 1)
                elif e[0] == "ot":
                    _, g, half = e
                    wait_filled(dve, e)
                    if g:
                        dve.wait_ge(attn_added, ot_count[g - 1, half])
                    o = bank(e).rearrange("p (t h d) -> p t h d", t=CT, h=HG)
                    link(nc.vector.reciprocal(inv_sum[:, half, :, :], o[:, :, :, HEAD_DIM]))
                    ins = nc.vector.tensor_tensor(
                        attn[:, half, :, :, :], o[:, :, :, 0:HEAD_DIM],
                        inv_sum[:, half, :, :].unsqueeze(3).to_broadcast([P, CT, HG, HEAD_DIM]), ALU.mult)
                    drained(ins, e)
                elif e[0] == "scale":
                    c = e[1]
                    src, n = quant_blocks(c)
                    if c == "w":
                        dve.wait_ge(wffn_loaded, 16)
                    if quant_count[c] > 1:
                        dve.wait_ge(dequantized, quant_count[c] - 1)
                    link(nc.vector.tensor_reduce(amax[:, 0:n], src, axis=AX.X, op=ALU.max,
                                                 apply_absolute_value=True))
                    link(nc.vector.tensor_scalar(qscale[:, 0:n], amax[:, 0:n], 1.0 / FP8_MAX, None, ALU.mult))
                    nc.vector.reciprocal(qinv[:, 0:n], qscale[:, 0:n]).then_inc(scales_ready, 1)
                elif e[0] == "expo":
                    c = e[1]
                    v, n = quant_blocks(c)
                    dve.wait_ge(scaled_ready, quant_count[c])
                    link(nc.vector.tensor_scalar(qexp[:, 0:n, :].bitcast(U32), v.bitcast(U32), 0x7F800000,
                                                 None, ALU.bitwise_and))
                    nc.vector.tensor_scalar(qexp[:, 0:n, :], qexp[:, 0:n, :], FP8_LEAST_NORMAL, ROUND_3_BITS,
                                            ALU.max, ALU.mult).then_inc(exponents_ready, 1)
                elif e[0] == "ffn":
                    _, c, pair = e
                    t0 = c * CT + 2 * pair
                    wait_filled(dve, e)
                    v = xs[:, t0:t0 + 2, :]
                    earlier = [k for k in ot_count if (k[0] // GPB, k[1]) == (c // CPB, c % CPB)
                               and at[("ot",) + k] < at[e]]
                    if earlier:
                        dve.wait_ge(attn_added, max(ot_count[k] for k in earlier))
                    ins = nc.vector.tensor_tensor(v, bank(e).rearrange("p (t n) -> p t n", t=2), v, ALU.add)
                    drained(ins, e)

        @block.tensor
        def _(pe):
            pe.wait_ge(consts_set, 1)
            pe.wait_ge(psum_cleared, 1)
            for e in order:
                if e[0] == "xt":
                    _, c, eh = e
                    pe.wait_ge(xn_ready, chunk_count[c])
                    wait_free(pe, e)
                    for t in range(CT):
                        ins = nc.tensor.transpose(bank(e)[:, t * P:(t + 1) * P],
                                                  xn[:, c * CT + t, eh * P:(eh + 1) * P], ident[:, :])
                    filled(ins, e)
                elif e[0] == "ckv":
                    c = e[1]
                    for eh in range(EH):
                        wait_drained(pe, ("xt", c, eh))
                    if c == 0:
                        pe.wait_ge(w_loaded, 64)
                    wait_free(pe, e)
                    for eh in range(EH):
                        ins = nc.tensor.matmul(bank(e)[0:LATENT, :], wkd_sb[:, eh, :], xnt[:, c % 2, eh, :],
                                               start=(eh == 0), stop=(eh == EH - 1))
                    filled(ins, e)
                elif e[0] == "proj":
                    _, t, c, ab = e
                    wait_free(pe, e)
                    if t == 0:
                        for eh in range(EH):
                            ins = nc.tensor.matmul(bank(e), wq_sb[:, eh, ab * P:(ab + 1) * P],
                                                   xnt[:, c % 2, eh, :], start=(eh == 0), stop=(eh == EH - 1))
                    else:
                        wait_drained(pe, ("ckv", c))
                        ins = nc.tensor.matmul(bank(e), wku_sb[:, ab * P:(ab + 1) * P], ckvt[:, c % 2, :],
                                               start=True, stop=True)
                    filled(ins, e)
                elif e[0] == "v":
                    _, c, pair = e
                    wait_drained(pe, ("ckv", c))
                    wait_free(pe, e)
                    for t in range(2):
                        tok = (2 * pair + t) * P
                        ins = nc.tensor.matmul(bank(e)[:, t * EMBED:(t + 1) * EMBED], ckvt[:, c % 2, tok:tok + P],
                                               wv_sb[:, :], start=True, stop=True)
                    filled(ins, e)
                elif e[0] == "s":
                    _, g, u = e
                    if u == 0:
                        pe.wait_ge(kq_loaded[g % KQ_SLOTS], 16 * 12 * (g // KQ_SLOTS + 1))
                    wait_free(pe, e)
                    unit, k = UNITS[u], g % KQ_SLOTS
                    first, col = True, 0
                    for h, i, j, n in unit:
                        if j <= i < j + n and not (n == 1 and col):
                            at0 = col + (i - j) * P
                            w = 4 * P if n == 1 else P
                            nc.tensor.matmul(bank(e)[:, at0:at0 + w], ident_bf[:, :],
                                             mask_bf[:, 0:w // P, :].rearrange("p a n -> p (a n)"),
                                             start=first, stop=False, skip_group_check=True)
                            first = False
                        col += n * P
                    col = 0
                    for h, i, j, n in unit:
                        ins = nc.tensor.matmul(bank(e)[:, col:col + n * P], qt[0:SPLIT_ROWS, k, h, i * P:(i + 1) * P],
                                               kt[0:SPLIT_ROWS, k, h, j * P:(j + n) * P], start=first, stop=True,
                                               skip_group_check=True)
                        first = False
                        col += n * P
                    filled(ins, e)
                elif e[0] == "shift":
                    pe.wait_ge(shift_split, e[1] + 1)
                    wait_free(pe, e)
                    n = 2 * HG * SEQ_TILES
                    filled(nc.tensor.transpose(bank(e)[0:n, 0:P // 2].bitcast(BF16), shift_parts[:, :],
                                               ident_bf[:, :]), e)
                elif e[0] == "t":
                    _, g, q, h = e
                    if q == 0 and h == 0:
                        pe.wait_ge(shift_placed, 32 * (g + 1))
                    wait_free(pe, e)
                    k, col = g % KQ_SLOTS, 0
                    for _, j, q0, n in QUADS[q]:
                        ins = nc.tensor.matmul(bank(e)[:, col:col + n * P], kt[:, k, h, j * P:(j + 1) * P],
                                               qt[:, k, h, q0 * P:(q0 + n) * P], start=True, stop=True)
                        col += n * P
                    filled(ins, e)
                elif e[0] == "pv":
                    _, g, q = e
                    b = g // GPB
                    n = quads[g, q]
                    wait_drained(pe, ("t", g, q, HG - 1))
                    if DIAGONALS[q]:
                        pe.wait_ge(probs_zeroed, diag_count[g, q])
                    for half in range(2):
                        if q == HALF_FIRST[half]:
                            wait_free(pe, ("o", g, half))
                    col = 0
                    for s, (half, j, q0, w) in enumerate(QUADS[q]):
                        c0 = (q0 - half * CT) * P
                        for h in range(HG):
                            ins = nc.tensor.matmul(
                                ps[32 * h:32 * h + 17, BANKS_O[half], c0:c0 + w * P],
                                v_sb[:, b, j, (g % GPB) * HG + h, :],
                                probs[:, n % PR, h, col:col + w * P],
                                start=(q == HALF_FIRST[half]), stop=(q == HALF_LAST[half]), skip_group_check=True)
                        col += w * P
                        if s == len(QUADS[q]) - 1:
                            ins.then_inc(pv_done, 1)
                elif e[0] == "ot":
                    _, g, half = e
                    wait_drained(pe, ("o", g, half))
                    wait_free(pe, e)
                    for t in range(CT):
                        ins = nc.tensor.transpose(bank(e)[:, t * P:(t + 1) * P], o_sb[:, half, t * P:(t + 1) * P],
                                                  ident[:, :])
                    filled(ins, e)
                elif e[0] == "xdt":
                    _, c, k = e
                    pe.wait_ge(dequantized, quant_count[c])
                    wait_free(pe, e)
                    for t in range(CT):
                        ins = nc.tensor.transpose(bank(e)[:, t * P:(t + 1) * P], xn[:, c * CT + t, k * P:(k + 1) * P], ident[:, :])
                    filled(ins, e)
                elif e[0] == "wt":
                    pe.wait_ge(dequantized, quant_count["w"])
                    wait_free(pe, e)
                    for k in range(EH):
                        for a in range(EH):
                            ins = nc.tensor.transpose(bank(e)[:, (k * EH + a) * P:(k * EH + a + 1) * P],
                                                      w_sb[:, a, k * P:(k + 1) * P], ident[:, :])
                    filled(ins, e)
                elif e[0] == "ffn":
                    _, c, pair = e
                    for k in range(EH):
                        wait_drained(pe, ("xdt", c, k))
                    wait_drained(pe, ("wt",))
                    wait_free(pe, e)
                    for t in range(2):
                        tok = (2 * pair + t) * P
                        for k in range(EH):
                            ins = nc.tensor.matmul(bank(e)[:, t * EMBED:(t + 1) * EMBED], xnt[:, c % 2, k, tok:tok + P],
                                                   wt[:, k, :], start=(k == 0), stop=(k == EH - 1))
                    filled(ins, e)


def rope_tables():
    import numpy as np
    freqs = np.float32(1.0) / np.power(np.float32(THETA), np.arange(0, ROPE, 2, dtype=np.float32) / np.float32(ROPE))
    angle = freqs.astype(np.float32)[:, None] * np.arange(SEQ, dtype=np.float32)[None, :]
    still = np.zeros((NOPE // 2, SEQ), np.float32)
    angle = np.concatenate([still, angle]).astype(np.float32)
    return np.cos(angle).astype(np.float32), np.sin(angle).astype(np.float32)


def column_order():
    first = list(range(NOPE // 2)) + list(range(NOPE, HEAD_DIM, 2))
    second = list(range(NOPE // 2, NOPE)) + list(range(NOPE + 1, HEAD_DIM, 2))
    return [h * HEAD_DIM + d for dims in (first, second) for d in dims for h in range(HEADS)]


def kernel(**inputs):
    import numpy as np
    import concourse.bacc as bacc
    from concourse.bass_utils import run_bass_kernel_spmd

    cos, sin = rope_tables()
    cols = column_order()
    arrays = {
        "x": np.ascontiguousarray(inputs["L0_attn_x"]),
        "wq": np.ascontiguousarray(np.asarray(inputs["L0_attn_Wq"])[:, cols]),
        "wkd": np.ascontiguousarray(inputs["L0_attn_Wkv_down"]),
        "wku": np.ascontiguousarray(np.asarray(inputs["L0_attn_Wk_up"])[:, cols]),
        "wv": np.ascontiguousarray(inputs["L0_attn_Wv_up"]),
        "wffn": np.ascontiguousarray(inputs["L0_ffn_weight"]),
        "cos": cos,
        "sin": sin,
    }
    nc = bacc.Bacc("TRN2", target_bir_lowering=False, num_devices=1)
    aps = {n: nc.dram_tensor(n, a.shape, mybir.dt.from_np(a.dtype), kind="ExternalInput").ap()
           for n, a in arrays.items()}
    out = nc.dram_tensor("out", (BATCH, SEQ, EMBED), F32, kind="ExternalOutput").ap()
    build(nc, *aps.values(), out)
    r = run_bass_kernel_spmd(nc, [arrays], core_ids=[0])
    return r.results[0]["out"]
```

```python
from contextlib import ExitStack

import concourse.bass as bass
from concourse import mybir

ALU = mybir.AluOpType
ACT = mybir.ActivationFunctionType
AX = mybir.AxisListType
F32 = mybir.dt.float32
BF16 = mybir.dt.bfloat16
U32 = mybir.dt.uint32

P = 128
BATCH, SEQ, EMBED = 2, 1024, 256
HEADS, LATENT = 16, 64
HEAD_DIM = EMBED // HEADS
NOPE = HEAD_DIM // 4
ROPE = HEAD_DIM - NOPE
SCALE = HEAD_DIM ** -0.5
LN_EPS = 1e-5
THETA = 10000.0

TILES = BATCH * SEQ // P
SEQ_TILES = SEQ // P
CHUNK = 512
CT = CHUNK // P
CHUNKS = BATCH * SEQ // CHUNK
CPB = SEQ // CHUNK
HG = 4
GPB = HEADS // HG
HALF = HEAD_DIM // 2
EH = EMBED // P

PARTS = 3
Q_SLOTS = [0, 0, 0, 1, 1, 2]
K_SLOTS = [0, 1, 2, 0, 1, 0]
assert K_SLOTS == [k for part in range(PARTS) for k in range(Q_SLOTS.count(part))]
SPLIT_ROWS = len(Q_SLOTS) * HEAD_DIM
ALL_ROWS = SPLIT_ROWS + 2
VC = HEAD_DIM + 1

QBLOCK = 128
FP8_MAX = 448.0
FP8_LEAST_NORMAL = 2.0 ** -6
ROUND_3_BITS = 1.5 * 2.0 ** 20
MASKED = -1e30
LOWEST = -3e38
TWO_BF16_ONES = 1.0 + 0x3F80 / 2.0 ** 23

NS, NT, NA = 3, 2, 2
BANKS_S = list(range(NS))
BANKS_T = list(range(NS, NS + NT))
BANK_O = NS + NT
BANKS_A = list(range(BANK_O + 1, BANK_O + 1 + NA))
CHUNK_ORDER = (0, 1, 3, 2)
KQ_SLOTS = 4
PR = 3
LOADS = 3
FIRST_LEAD = 6
LEAD = 8
MOST_UNITS = 3
SHIFT_LAG = 3
INTERLUDE = 26
POOL_CHUNKS = CPB
FRONT_GAP = 8
FFN_START, FFN_GAP = 15, 8
FFN_IDLE = 5

STAGES = [(c, g) for c in CHUNK_ORDER for g in range(GPB)]
NSTAGES = len(STAGES)


def max_units(half):
    fours, twos, ones = (([(3, 0)], [(1, 0), (2, 0)], [(0, 0), (2, 2)]),
                         ([(7, 0), (7, 4), (4, 0), (5, 0), (6, 0)], [(5, 4), (6, 4)], [(4, 4), (6, 6)]))[half]
    units = [[(h, i, j, 4)] for i, j in fours for h in range(HG)]
    units += [[(h, i, j, 2) for h in (hp, hp + 1)] for i, j in twos for hp in (0, 2)]
    units += [[(h, i, j, 1) for h in range(HG)] for i, j in ones]
    return units


QUADS = [[([(0, 0, 4)], 1), ([(1, 1, 3), (3, 3, 1)], 1), ([(2, 2, 2)], 2)],
         [([(0, 4, 4)], 1), ([(1, 4, 4)], 1), ([(2, 4, 4)], 1), ([(3, 4, 4)], 1), ([(4, 4, 4)], 1),
          ([(5, 5, 3), (7, 7, 1)], 1), ([(6, 6, 2)], 2)]]
UNITS = [max_units(half) for half in range(2)]


def half_of(stage):
    return STAGES[stage][0] % CPB


def diagonals(half, q):
    out, col = [], 0
    for j, q0, n in QUADS[half][q][0]:
        if q0 == j:
            out.append(col)
        col += n * P
    return out


def plan():
    order = [
        ("stats", 0), ("root", 0), ("norm", 0), ("stats", 1), ("root", 1), ("xt", 0, 0), ("xt", 0, 1), ("norm", 1),
        ("proj", 0, 0, 0), ("proj", 0, 0, 1), ("rope", 0, 0), ("ckv", 0), ("stats", 2), ("root", 2),
        ("part1", 0, 0), ("xt", 1, 0), ("xt", 1, 1), ("proj", 1, 0, 0), ("proj", 1, 0, 1), ("rope", 1, 0),
        ("v", 0, 0), ("rest", 0, 0), ("part2", 0, 0), ("part1", 1, 0), ("part3", 0, 0), ("proj", 0, 1, 0),
        ("rest", 1, 0), ("part2", 1, 0), ("norm", 2), ("part3", 1, 0), ("proj", 0, 1, 1), ("rope", 0, 1),
        ("ckv", 1), ("v", 0, 1), ("xt", 2, 0), ("xt", 2, 1), ("part1", 0, 1), ("stats", 3), ("root", 3),
        ("proj", 1, 1, 0), ("proj", 1, 1, 1), ("rope", 1, 1), ("v", 1, 0), ("v", 1, 1), ("rest", 0, 1),
        ("part2", 0, 1), ("part1", 1, 1), ("part3", 0, 1)]
    for e in [e for e in order if e[0] in ("part1", "part2", "part3")]:
        order.insert(order.index(e) + 1, ("store", e[1], e[2], int(e[0][-1]) - 1))
    for s in range(2):
        place = order.index(("store", 1, 0, 1 + s)) + 1
        order[place:place] = [("load", s, 0, n) for n in range(LOADS)]
    place = order.index(("load", 1, 0, 0))
    order[place:place] = [("load", 0, 1, n) for n in range(LOADS)]
    order += [("load", 1, 1, n) for n in range(LOADS)]
    order += [("load", 2, t, n) for t in range(2) for n in range(LOADS)]
    between = {INTERLUDE: [("rest", 1, 1), ("part2", 1, 1), ("store", 1, 1, 1)], INTERLUDE + 1: [("part3", 1, 1)],
               INTERLUDE + 2: [("norm", 3), ("store", 1, 1, 2)]}

    jobs = []
    for n, c in enumerate(range(CPB, CHUNKS)):
        transposes = [] if c == CPB else [[("xt", c, 0)], [("xt", c, 1)]]
        jobs.append((FRONT_GAP * n, transposes + [
            [("proj", 0, c, 0)], [("proj", 0, c, 1)], [("rope", 0, c), ("ckv", c)],
            [("part1", 0, c), ("proj", 1, c, 0)], [("rest", 0, c), ("proj", 1, c, 1), ("store", 0, c, 0)],
            [("rope", 1, c), ("part2", 0, c)], [("part3", 0, c), ("part1", 1, c), ("v", c, 0), ("store", 0, c, 1)],
            [("v", c, 1), ("rest", 1, c), ("store", 0, c, 2), ("store", 1, c, 0)], [("part2", 1, c)],
            [("part3", 1, c), ("store", 1, c, 1)], [("store", 1, c, 2)]]))
    for n, c in enumerate(["w"] + list(range(CHUNKS))):
        fp8 = [[("scale", c)], [("quant", c)], [("expo", c)], [("round", c)], [("squeeze", c)], []]
        if c == "w":
            use = [[("wt",)], [("wscale",)]]
        else:
            use = [[("xdt", c)], *[[]] * FFN_IDLE, [("ffn", c, 0)],
                   *[[("ffn", c, t), ("fadd", c, t - 1)] for t in range(1, CT)], [("fadd", c, CT - 1)]]
        jobs.append((FFN_START + FFN_GAP * n, fp8 + use))
    side = [[e for start, pieces in jobs if start <= n < start + len(pieces) for e in pieces[n - start]]
            for n in range(max(start + len(pieces) for start, pieces in jobs))]

    maxima = [(s, u) for s in range(NSTAGES) for u in range(len(UNITS[half_of(s)]))]
    all_units = len(maxima)
    shifts = []

    def next_maximum():
        if maxima:
            order.extend(between.pop(all_units - len(maxima), []))
            s, u = maxima.pop(0)
            order.append(("s", s, u))
            if u == len(UNITS[half_of(s)]) - 1:
                order.append(("max", s))
                shifts.append([SHIFT_LAG + 1, s])
        for waiting in list(shifts):
            waiting[0] -= 1
            if waiting[0] == 0:
                order.append(("shift", waiting[1]))
                if waiting[1] + 3 < KQ_SLOTS:
                    order.extend(("load", waiting[1] + 3, t, n) for n in range(LOADS) for t in range(2))
                shifts.remove(waiting)

    for n in range(len(UNITS[0]) + FIRST_LEAD):
        next_maximum()
    due, units, banks = [], 0, 0
    for s in range(NSTAGES):
        units += len(UNITS[half_of(s)])
        due.append((units, banks - (LEAD if s > 1 else FIRST_LEAD)))
        banks += sum(HG // heads for _, heads in QUADS[half_of(s)])
    made, bank_no, credit = len(UNITS[0]) + FIRST_LEAD, 0, 0.0
    steps = [(s, q) for s in range(NSTAGES) for q in range(len(QUADS[half_of(s)]))]
    loads = []
    for n, (s, q) in enumerate(steps):
        for u in range(HG // QUADS[half_of(s)][q][1]):
            credit += max([(units - made) / (by - bank_no) for units, by in due if by > bank_no], default=0)
            for _ in range(MOST_UNITS):
                if credit > 1e-6 and maxima and ("load", maxima[0][0], 1, LOADS - 1) in order:
                    next_maximum()
                    credit, made = credit - 1, made + 1
            if not maxima:
                next_maximum()
            bank_no += 1
            order.append(("t", s, q, u))
            if u == 1 and n >= 2:
                order.append(("pv",) + steps[n - 2])
                if steps[n - 1][1] == 0:
                    order.append(("oev", steps[n - 2][0]))
        if diagonals(half_of(s), q):
            order.append(("diag", s, q))
        if loads and ("store", 1, STAGES[loads[0][1]][0], PARTS - 1) in order:
            order.append(loads.pop(0))
            for _ in range(3 - 2 * half_of(s)):
                if loads:
                    order.append(loads.pop(0))
        if q == len(QUADS[half_of(s)]) - 1 and s + KQ_SLOTS < NSTAGES:
            loads += [("load", s + KQ_SLOTS, t, n) for n in range(LOADS) for t in range(2)]
        if n >= 3 and steps[n - 2][1] == 0:
            order.append(("ot", steps[n - 3][0]))
        elif side:
            order += side.pop(0)
    assert not side and not maxima and not loads, (len(side), len(maxima), len(loads))
    s, q = steps[-1]
    order += [("pv", s, q - 1), ("pv", s, q), ("oev", s), ("ot", s)]
    for c in range(CHUNKS):
        last = [("ot", STAGES.index((c, GPB - 1))), ("fadd", c, CT - 1)]
        order.insert(max(order.index(e) for e in last) + 1, ("out", c))
    return order


def build(nc, x, wq, wkd, wku, wv, wffn, cos, sin, out):
    order = plan()
    at = {e: n for n, e in enumerate(order)}
    assert len(at) == len(order)

    filling, fillings, turn = {}, [0] * 8, {"s": 0, "t": 0, "a": 0}

    def take(key, kind, banks):
        b = banks[turn[kind] % len(banks)]
        turn[kind] += 1
        filling[key] = (b, fillings[b])
        fillings[b] += 1

    for e in order:
        if e[0] == "s":
            take(e, "s", BANKS_S + BANKS_T if at[e] < at["t", 0, 0, 0] else BANKS_S)
        elif e[0] == "t":
            take(e, "t", BANKS_T)
        elif e[0] == "pv":
            if e[2] == len(QUADS[half_of(e[1])]) - 1:
                b = BANK_O
                filling["o", e[1]] = (b, fillings[b])
                fillings[b] += 1
        elif e[0] in ("proj", "xt", "ckv", "v", "shift", "ot", "xdt", "ffn", "wt", "wscale"):
            take(e, "a", BANKS_A + BANKS_S + BANKS_T if at[e] < at["s", 0, 0] else BANKS_A)
    quads = {e[1:3]: n for n, e in enumerate(e for e in order if e[0] == "t" and e[3] == 0)}
    last_unit = {e[1:3]: e for e in order if e[0] == "t"}
    diag_count = {e[1:]: n + 1 for n, e in enumerate(e for e in order if e[0] == "diag")}
    pv_count = {e[1]: n + 1 for n, e in enumerate(e for e in order if e[0] == "pv")}
    splits = [e[1:3] for e in order if e[0] == "proj" and e[3] == 0]
    split_count = {e: n + 1 for n, e in enumerate(splits)}
    chunk_count = {e[1]: n + 1 for n, e in enumerate(e for e in order if e[0] == "stats")}
    quant_transposed = [("wt",) if e[1] == "w" else ("xdt", e[1]) for e in order if e[0] == "scale"]
    ffn_entries = [e for e in order if e[0] == "ffn"]
    ffn_count = {e[1:]: n + 1 for n, e in enumerate(e for e in order if e[0] == "ffn")}
    quant_count = {e[1]: n + 1 for n, e in enumerate(e for e in order if e[0] == "scale")}

    with ExitStack() as ctx:
        def sb(name, shape, dt=F32):
            return ctx.enter_context(nc.sbuf_tensor(name, shape, dt))

        def sem(name):
            return ctx.enter_context(nc.semaphore(name))

        xs = sb("xs", [P, TILES, EMBED])
        wq_sb = sb("wq_sb", [P, EH, EMBED])
        wkd_sb = sb("wkd_sb", [P, EH, LATENT])
        wku_sb = sb("wku_sb", [LATENT, EMBED])
        wv_sb = sb("wv_sb", [LATENT, EMBED])
        w_sb = sb("w_sb", [P, EH, EMBED])
        cos_sb = sb("cos_sb", [P, SEQ])
        sin_sb = sb("sin_sb", [P, SEQ])
        ident = sb("ident", [P, P])
        ident_bf = sb("ident_bf", [P, P], BF16)
        mask_bf = sb("mask_bf", [P, 4, P], BF16)
        stats = sb("stats", [P, CT, 6])
        moments = sb("moments", [P, TILES, 2])
        variance = sb("variance", [P, TILES])
        deviation = sb("deviation", [P, TILES])
        rstd = sb("rstd", [P, TILES])
        newton = sb("newton", [P, TILES])
        xn = sb("xn", [P, TILES, EMBED])
        xnt = sb("xnt", [P, 2, EH, CHUNK])
        ckvt = sb("ckvt", [LATENT, 2, CHUNK])
        rope_products = sb("rope_products", [P, 2, 4, CHUNK])
        ffn_sb = rope_products[:, 0, :, :]
        quantized = rope_products[:, 1, :, :].rearrange("p a n -> p (a n)").bitcast(BF16)\
            .rearrange("p (r a n) -> p r a n", r=4, n=QBLOCK)
        rotated = sb("rotated", [P, 2, 2, CHUNK])
        rest = sb("rest", [P, 2, 2, CHUNK])
        parts = sb("parts", [P, 2, PARTS, 2, CHUNK], BF16)
        v_sb = sb("v_sb", [P, BATCH, SEQ_TILES, HEADS, VC])
        qt = sb("qt", [ALL_ROWS, KQ_SLOTS, HG, CHUNK], BF16)
        kt = sb("kt", [ALL_ROWS, KQ_SLOTS, CPB, HG, CHUNK], BF16)
        block_max = sb("block_max", [P, CPB, HG, CT, SEQ_TILES])
        neg_max = sb("neg_max", [P, HG * CT])
        shift_parts = sb("shift_parts", [P, 2 * HG * CT], BF16)
        shift_t = sb("shift_t", [2 * HG * CT, P], BF16)
        probs = sb("probs", [P, PR, HG, CHUNK])
        o_sb = sb("o_sb", [P, 2, CHUNK])
        inv_sum = sb("inv_sum", [P, 2, CT, HG])
        attn = sb("attn", [P, 2, CT, HG, HEAD_DIM])
        amax = sb("amax", [P, 8])
        qscale = sb("qscale", [P, 3, 8])
        qinv = sb("qinv", [P, 8])
        qexp = sb("qexp", [P, 8, QBLOCK])
        wt = wq_sb[:, 0, :].bitcast(BF16).rearrange("p (k n) -> p k n", k=EH)
        w_scales = w_sb

        def xdt(c):
            return xnt[:, c % 2, 0, :].bitcast(BF16).rearrange("p (k n) -> p k n", k=EH)

        def scales_of(c, n):
            return qscale[:, 2 if c == "w" else c % 2, 0:n]

        ps = ctx.enter_context(nc.psum_tensor("ps", [P, 8, 512], F32))
        scratch = nc.dram_tensor("split_scratch", [2, CHUNKS, PARTS, 2, P, CHUNK], BF16).ap()

        bank_filled = [sem(f"bank_filled{b}") for b in range(8)]
        bank_drained = [sem(f"bank_drained{b}") for b in range(8)]
        x_loaded = [sem(f"x_loaded{c}") for c in range(CHUNKS)]
        wq_loaded = sem("wq_loaded")
        w_loaded = sem("w_loaded")
        wffn_loaded = sem("wffn_loaded")
        tables_loaded = sem("tables_loaded")
        consts_set = sem("consts_set")
        psum_cleared = sem("psum_cleared")
        dve_chain = sem("dve_chain")
        pool_chain = sem("pool_chain")
        var_ready = sem("var_ready")
        dev_ready = sem("dev_ready")
        xn_ready = sem("xn_ready")
        first_rotated = sem("first_rotated")
        second_rotated = sem("second_rotated")
        part1_ready = sem("part1_ready")
        rest_ready = sem("rest_ready")
        part2_ready = sem("part2_ready")
        part3_ready = sem("part3_ready")
        parts_stored = {(t, c): sem(f"parts_stored{t}_{c}") for t in range(2) for c in range(CHUNKS)}
        kq_loaded = [sem(f"kq_loaded{k}") for k in range(KQ_SLOTS)]
        shift_split = sem("shift_split")
        shift_placed = sem("shift_placed")
        probs_zeroed = sem("probs_zeroed")
        pv_done = sem("pv_done")
        attn_added = sem("attn_added")
        ffn_first = sem("ffn_first")
        ffn_added = sem("ffn_added")
        scales_ready = sem("scales_ready")
        scaled_ready = sem("scaled_ready")
        exponents_ready = sem("exponents_ready")
        raised = sem("raised")
        rounded = sem("rounded")
        out_stored = sem("out_stored")

        def bank(key):
            return ps[:, filling[key][0], :]

        def wait_filled(eng, key):
            b, n = filling[key]
            eng.wait_ge(bank_filled[b], n + 1)

        def wait_free(eng, key):
            b, n = filling[key]
            if n:
                eng.wait_ge(bank_drained[b], n)

        def wait_drained(eng, key):
            b, n = filling[key]
            eng.wait_ge(bank_drained[b], n + 1)

        def filled(ins, key):
            ins.then_inc(bank_filled[filling[key][0]], 1)

        def drained(ins, key):
            ins.then_inc(bank_drained[filling[key][0]], 1)

        def quant_blocks(c):
            if c == "w":
                return w_sb[:, :, :].rearrange("p a (k f) -> p (a k) f", f=QBLOCK), EH * EMBED // QBLOCK
            return (xn[:, c * CT:(c + 1) * CT, :].rearrange("p a (k f) -> p (a k) f", f=QBLOCK),
                    CT * EMBED // QBLOCK)

        def rotate(eng, unit, e, first):
            n = split_count[e[1:]]
            products, to = rope_products[:, n % 2, :, :], rotated[:, n % 2, :, :]
            wait_drained(eng, ("proj",) + e[1:] + (1,))
            if n > 2:
                eng.wait_ge(rest_ready, n - 2)
            if first:
                unit.tensor_tensor(to[:, 0, :], products[:, 0, :], products[:, 3, :], ALU.subtract)\
                    .then_inc(first_rotated, 1)
            else:
                unit.tensor_tensor(to[:, 1, :], products[:, 2, :], products[:, 1, :], ALU.add)\
                    .then_inc(second_rotated, 1)

        def remainder(eng, unit, e):
            n = split_count[e[1:]]
            eng.wait_ge(part1_ready, n)
            if n > 2:
                eng.wait_ge(part3_ready, n - 2)
            unit.tensor_tensor(rest[:, n % 2, :, :], rotated[:, n % 2, :, :], parts[:, n % 2, 0, :, :],
                               ALU.subtract).then_inc(rest_ready, 1)

        block = ctx.enter_context(nc.Block())

        @block.sync
        def _(sp):
            xv = x.rearrange("b (t p) e -> p (b t) e", p=P)
            def load_x(c):
                sp.dma_start(xs[:, c * CT:(c + 1) * CT, :], xv[:, c * CT:(c + 1) * CT, :]).then_inc(x_loaded[c], 16)

            load_x(0)
            sp.dma_start(wq_sb[:, :, :], wq.rearrange("(a p) n -> p a n", p=P)).then_inc(wq_loaded, 16)
            load_x(1)
            sp.dma_start(wkd_sb[:, :, :], wkd.rearrange("(a p) n -> p a n", p=P)).then_inc(w_loaded, 16)
            sp.dma_start(wku_sb[:, :], wku).then_inc(w_loaded, 16)
            sp.dma_start(wv_sb[:, :], wv).then_inc(w_loaded, 16)
            for dst, src in ((cos_sb, cos), (sin_sb, sin)):
                rows = bass.AP(src.tensor, src.offset, [[SEQ, HALF], [0, HEADS], [1, SEQ]])
                sp.dma_start(dst[:, :], rows).then_inc(tables_loaded, 16)
            for c in range(2, CHUNKS):
                load_x(c)
            sp.dma_start(w_sb[:, :, :], wffn.rearrange("(a p) n -> p a n", p=P)).then_inc(wffn_loaded, 16)
            outs = 0
            for e in order:
                if e[0] == "store":
                    _, t, c, part = e
                    n = split_count[t, c]
                    sp.wait_ge((part1_ready, part2_ready, part3_ready)[part], n)
                    sp.dma_start(scratch[t, c, part].rearrange("a p n -> p a n"),
                                 parts[:, n % 2, part, :, :]).then_inc(parts_stored[t, c], 16)
                elif e[0] == "load":
                    _, s, t, portion = e
                    c, g = STAGES[s]
                    half = c % CPB
                    copies, row0 = Q_SLOTS.count(portion), Q_SLOTS.index(portion) * HEAD_DIM
                    rows = slice(row0, row0 + copies * HEAD_DIM)
                    row = HEADS * CHUNK
                    if s >= KQ_SLOTS and t == 0 and portion == 0:
                        wait_filled(sp, last_unit[s - KQ_SLOTS, len(QUADS[half_of(s - KQ_SLOTS)]) - 1])
                    if t == 0:
                        sp.wait_ge(parts_stored[0, c], 16 * PARTS)
                        src = scratch[0, c, portion, 0, g * HG, :]
                        src = bass.AP(src.tensor, src.offset, [[0, copies], [row, HEAD_DIM], [1, HG * CHUNK]])
                        dst = qt[rows, s % KQ_SLOTS, :, :]
                    else:
                        for k in range(half + 1):
                            sp.wait_ge(parts_stored[1, c - k], 16 * PARTS)
                        src = scratch[1, c - half, 0, 0, g * HG, :]
                        src = bass.AP(src.tensor, src.offset, [[row, copies * HEAD_DIM],
                                                               [PARTS * HEAD_DIM * row, half + 1], [1, HG * CHUNK]])
                        dst = kt[rows, s % KQ_SLOTS, 0:half + 1, :, :]
                    sp.dma_start(dst, src).then_inc(kq_loaded[s % KQ_SLOTS], 16)
                elif e[0] == "shift":
                    s, n = e[1], HG * CT
                    wait_drained(sp, e)
                    for part in range(2):
                        row = SPLIT_ROWS + part
                        sp.dma_start(qt[row:row + 1, s % KQ_SLOTS, :, :].rearrange("p h (i n) -> p (h i) n", n=P),
                                     shift_t[part * n:(part + 1) * n, :]).then_inc(shift_placed, 16)
                elif e[0] == "out":
                    c = e[1]
                    sp.wait_ge(attn_added, STAGES.index((c, GPB - 1)) + 1)
                    sp.wait_ge(ffn_added, ffn_count[c, CT - 1])
                    sp.dma_start(out.rearrange("b (t p) e -> p (b t) e", p=P)[:, c * CT:(c + 1) * CT, :],
                                 xs[:, c * CT:(c + 1) * CT, :]).then_inc(out_stored, 16)
                    outs += 16
            sp.wait_ge(out_stored, outs)

        @block.gpsimd
        def _(pool):
            chain = [0]

            def link(ins):
                chain[0] += 1
                ins.then_inc(pool_chain, 1)
                pool.wait_ge(pool_chain, chain[0])

            nc.gpsimd.memset(ident[:, :], 0.0)
            nc.gpsimd.memset(ident_bf[:, :], 0.0)
            nc.gpsimd.memset(mask_bf[:, :, :], 0.0)
            link(nc.gpsimd.memset(v_sb[:, :, :, :, HEAD_DIM:VC], 1.0))
            ones = kt[SPLIT_ROWS:ALL_ROWS, :, :, :, :].rearrange("p s c h n -> p (s c h n)")
            link(nc.gpsimd.memset(ones.bitcast(F32), TWO_BF16_ONES))
            for m in (ident, ident_bf):
                nc.gpsimd.affine_select(out=m[:, :], in_=m[:, :], compare_op=ALU.not_equal, fill=1.0,
                                        base=0, pattern=[[-1, P]], channel_multiplier=1)
            nc.gpsimd.affine_select(out=mask_bf[:, :, :], in_=mask_bf[:, :, :], compare_op=ALU.is_ge, fill=MASKED,
                                    base=0, pattern=[[0, 4], [-1, P]], channel_multiplier=1).then_inc(consts_set, 1)
            for e in order:
                if e[0] == "rope":
                    if e[2] >= POOL_CHUNKS:
                        rotate(pool, nc.gpsimd, e, first=True)
                    rotate(pool, nc.gpsimd, e, first=False)
                elif e[0] == "rest" and e[2] >= POOL_CHUNKS:
                    remainder(pool, nc.gpsimd, e)
                elif e[0] == "part3":
                    n = split_count[e[1:]]
                    pool.wait_ge(part2_ready, n)
                    nc.gpsimd.tensor_tensor(parts[:, n % 2, 2, :, :], rest[:, n % 2, :, :], parts[:, n % 2, 1, :, :],
                                            ALU.subtract).then_inc(part3_ready, 1)
                elif e[0] == "diag":
                    _, s, q = e
                    wait_drained(pool, last_unit[s, q])
                    for col in diagonals(half_of(s), q):
                        v = probs[:, quads[s, q] % PR, :, col:col + P]
                        ins = nc.gpsimd.affine_select(out=v, in_=v, compare_op=ALU.is_ge, fill=0.0, base=0,
                                                      pattern=[[0, HG], [1, P]], channel_multiplier=-1)
                    ins.then_inc(probs_zeroed, 1)
                elif e[0] == "ot":
                    s = e[1]
                    c, g = STAGES[s]
                    t0, h0 = c * CT, g * HG
                    wait_drained(pool, e)
                    earlier = [k for k in order[:at[e]] if k[0] == "fadd"]
                    if earlier:
                        pool.wait_ge(ffn_added, len(earlier))
                    dst = xs[:, t0:t0 + CT, h0 * HEAD_DIM:(h0 + HG) * HEAD_DIM]
                    src = attn[:, s % 2, :, :, :].rearrange("p t h d -> p t (h d)")
                    nc.gpsimd.tensor_tensor(dst, dst, src, ALU.add).then_inc(attn_added, 1)
                elif e[0] == "fadd":
                    _, c, t = e
                    n = ffn_count[c, t]
                    v = xs[:, c * CT + t, :]
                    wait_drained(pool, ("ffn", c, t))
                    earlier = [s for s in range(NSTAGES) if at["ot", s] < at[e]]
                    if earlier:
                        pool.wait_ge(attn_added, earlier[-1] + 1)
                    share = ffn_sb[:, n % 4, 0:EMBED]
                    pool.wait_ge(ffn_first, n)
                    if n == 1:
                        wait_drained(pool, ("wscale",))
                    link(nc.gpsimd.tensor_tensor(share, share, w_scales[:, 0, :], ALU.mult))
                    link(nc.gpsimd.tensor_tensor(v, v, share, ALU.add))
                    nc.gpsimd.tensor_tensor(v, v, ffn_sb[:, n % 4, EMBED:2 * EMBED], ALU.add).then_inc(ffn_added, 1)
                elif e[0] == "quant":
                    c = e[1]
                    v, n = quant_blocks(c)
                    pool.wait_ge(scales_ready, quant_count[c])
                    nc.gpsimd.tensor_tensor(v, v,
                                            qinv[:, 0:n].unsqueeze(2).to_broadcast([P, n, QBLOCK]),
                                            ALU.mult).then_inc(scaled_ready, 1)
                elif e[0] == "round":
                    c = e[1]
                    v, n = quant_blocks(c)
                    pool.wait_ge(exponents_ready, quant_count[c])
                    nc.gpsimd.tensor_tensor(v, v, qexp[:, 0:n, :], ALU.add).then_inc(raised, 1)
                elif e[0] == "squeeze":
                    c = e[1]
                    v, n = quant_blocks(c)
                    pool.wait_ge(raised, quant_count[c])
                    m = quant_count[c]
                    if m > 2:
                        wait_filled(pool, quant_transposed[m - 3])
                    nc.gpsimd.tensor_tensor(quantized[:, m % 2, 0:n, :], v, qexp[:, 0:n, :], ALU.subtract)\
                        .then_inc(rounded, 1)

        @block.scalar
        def _(act):
            for e in order:
                if e[0] == "root":
                    c = e[1]
                    act.wait_ge(var_ready, chunk_count[c])
                    nc.scalar.activation(deviation[:, c * CT:(c + 1) * CT], variance[:, c * CT:(c + 1) * CT],
                                         ACT.Sqrt).then_inc(dev_ready, 1)
                elif e[0] == "xt":
                    _, c, eh = e
                    wait_filled(act, e)
                    if c >= 2:
                        wait_filled(act, ("proj", 0, c - 2, 1))
                        wait_filled(act, ("ckv", c - 2))
                    drained(nc.scalar.activation(xnt[:, c % 2, eh, :], bank(e), ACT.Copy), e)
                elif e[0] == "ckv":
                    wait_filled(act, e)
                    if e[1] >= 2:
                        wait_filled(act, ("proj", 1, e[1] - 2, 1))
                        wait_filled(act, ("v", e[1] - 2, 1))
                    drained(nc.scalar.activation(ckvt[:, e[1] % 2, :], bank(e)[0:LATENT, :], ACT.Copy), e)
                elif e[0] == "v":
                    _, c, pair = e
                    t0 = (c % CPB) * CT + 2 * pair
                    wait_filled(act, e)
                    if (c, pair) == (0, 0):
                        act.wait_ge(consts_set, 1)
                    drained(nc.scalar.activation(v_sb[:, c // CPB, t0:t0 + 2, :, 0:HEAD_DIM],
                                                 bank(e).rearrange("p (t h d) -> p t h d", t=2, h=HEADS),
                                                 ACT.Copy), e)
                elif e[0] == "part1":
                    n = split_count[e[1:]]
                    act.wait_ge(first_rotated, n)
                    act.wait_ge(second_rotated, n)
                    if n > 2:
                        act.wait_ge(parts_stored[splits[n - 3]], 16 * PARTS)
                    nc.scalar.activation(parts[:, n % 2, 0, :, :], rotated[:, n % 2, :, :], ACT.Copy)\
                        .then_inc(part1_ready, 1)
                elif e[0] == "part2":
                    n = split_count[e[1:]]
                    act.wait_ge(rest_ready, n)
                    nc.scalar.activation(parts[:, n % 2, 1, :, :], rest[:, n % 2, :, :], ACT.Copy)\
                        .then_inc(part2_ready, 1)
                elif e[0] == "shift":
                    wait_filled(act, e)
                    if e[1]:
                        act.wait_ge(shift_placed, 32 * e[1])
                    n = 2 * HG * CT
                    drained(nc.scalar.activation(shift_t[:, :], bank(e)[0:n, 0:P // 2].bitcast(BF16), ACT.Copy), e)
                elif e[0] == "t":
                    _, s, q, u = e
                    n = quads[s, q]
                    segments, heads = QUADS[half_of(s)][q]
                    w = CHUNK // heads
                    wait_filled(act, e)
                    if u == 0 and n >= PR:
                        act.wait_ge(pv_done, n - PR + 1)
                    drained(nc.scalar.activation(probs[:, n % PR, u * heads:(u + 1) * heads, 0:w],
                                                 bank(e).rearrange("p (h n) -> p h n", h=heads), ACT.Exp,
                                                 scale=SCALE), e)
                elif e[0] == "oev":
                    s = e[1]
                    act.wait_ge(pv_done, pv_count[s])
                    drained(nc.scalar.activation(o_sb[:, s % 2, :], bank(("o", s)), ACT.Copy), ("o", s))
                elif e[0] == "ffn":
                    _, c, t = e
                    n = ffn_count[c, t]
                    wait_filled(act, e)
                    if n == 1:
                        act.wait_ge(second_rotated, len(splits))
                    if n > 4:
                        act.wait_ge(ffn_added, n - 4)
                    nc.scalar.activation(ffn_sb[:, n % 4, 0:EMBED], bank(e)[:, 0:EMBED], ACT.Copy,
                                         scale=qscale[:, c % 2, t * EH:t * EH + 1]).then_inc(ffn_first, 1)
                elif e[0] in ("xdt", "wt"):
                    wait_filled(act, e)
                    if e[0] == "wt":
                        wait_filled(act, ("proj", 0, CHUNKS - 1, 1))
                        dst, n = wt, EH * EMBED // 2
                    else:
                        c = e[1]
                        for key in [("proj", 0, c + 2, 1), ("ckv", c + 2)] if c < 2 else [("ffn", c - 2, CT - 1)]:
                            wait_filled(act, key)
                        dst, n = xdt(c), EH * CHUNK // 2
                    drained(nc.scalar.activation(dst, bank(e)[:, 0:n].bitcast(BF16)
                                                 .rearrange("p (k n) -> p k n", k=EH), ACT.Copy), e)
                elif e[0] == "wscale":
                    wait_filled(act, e)
                    act.wait_ge(rounded, quant_count["w"])
                    drained(nc.scalar.activation(w_scales[:, :, :], bank(e).rearrange("p (k n) -> p k n", k=EH),
                                                 ACT.Copy), e)

        @block.vector
        def _(dve):
            chain = [0]

            def link(ins):
                chain[0] += 1
                ins.then_inc(dve_chain, 1)
                dve.wait_ge(dve_chain, chain[0])

            nc.vector.memset(block_max[:, :, :, :, :], LOWEST)
            nc.vector.memset(ps[:, BANK_O, :], 0.0).then_inc(psum_cleared, 1)
            for e in order:
                if e[0] == "stats":
                    c = e[1]
                    cs = slice(c * CT, (c + 1) * CT)
                    dve.wait_ge(x_loaded[c], 16)
                    for t in range(CT):
                        ins = nc.vector.bn_stats(stats[:, t, :], xs[:, c * CT + t, :])
                    link(ins)
                    for t in range(CT):
                        ins = nc.vector.bn_aggr(moments[:, c * CT + t, :], stats[:, t, :])
                    link(ins)
                    ins = nc.vector.tensor_scalar_add(variance[:, cs], moments[:, cs, 1], LN_EPS)
                    ins.then_inc(var_ready, 1)
                elif e[0] == "norm":
                    c = e[1]
                    cs = slice(c * CT, (c + 1) * CT)
                    dve.wait_ge(dev_ready, chunk_count[c])
                    link(nc.vector.reciprocal(rstd[:, cs], deviation[:, cs]))
                    link(nc.vector.tensor_tensor(newton[:, cs], rstd[:, cs], rstd[:, cs], ALU.mult))
                    link(nc.vector.tensor_tensor(newton[:, cs], newton[:, cs], variance[:, cs], ALU.mult))
                    link(nc.vector.tensor_scalar(newton[:, cs], newton[:, cs], -0.5, 1.5, ALU.mult, ALU.add))
                    link(nc.vector.tensor_tensor(rstd[:, cs], rstd[:, cs], newton[:, cs], ALU.mult))
                    for t in range(c * CT, (c + 1) * CT):
                        ins = nc.vector.tensor_scalar(xn[:, t, :], xs[:, t, :], moments[:, t, 0:1], rstd[:, t:t + 1],
                                                      ALU.subtract, ALU.mult)
                    ins.then_inc(xn_ready, 1)
                elif e[0] == "proj":
                    _, t, c, ab = e
                    n = split_count[t, c]
                    c0 = (c % CPB) * CHUNK
                    if n == 1:
                        dve.wait_ge(tables_loaded, 16 * 2)
                    if n > 2 and ab == 0:
                        dve.wait_ge(second_rotated, n - 2)
                    wait_filled(dve, e)
                    nc.vector.tensor_tensor(rope_products[:, n % 2, 2 * ab, :], bank(e), cos_sb[:, c0:c0 + CHUNK],
                                            ALU.mult)
                    drained(nc.vector.tensor_tensor(rope_products[:, n % 2, 2 * ab + 1, :], bank(e),
                                                    sin_sb[:, c0:c0 + CHUNK], ALU.mult), e)
                elif e[0] == "rope" and e[2] < POOL_CHUNKS:
                    rotate(dve, nc.vector, e, first=True)
                elif e[0] == "rest" and e[2] < POOL_CHUNKS:
                    remainder(dve, nc.vector, e)
                elif e[0] == "s":
                    _, s, u = e
                    half = half_of(s)
                    unit = UNITS[half][u]
                    h, i, j, n = unit[0]
                    wait_filled(dve, e)
                    to = block_max[:, half, h:h + len(unit), i - half * CT, j:j + n]
                    drained(nc.vector.tensor_reduce(
                        to, bank(e).rearrange("p (h j n) -> p h j n", h=len(unit), n=P), axis=AX.X, op=ALU.max), e)
                elif e[0] == "max":
                    s, half = e[1], half_of(e[1])
                    wait_drained(dve, ("s", s, len(UNITS[half]) - 1))
                    link(nc.vector.tensor_reduce(neg_max[:, :].rearrange("p (h i) -> p h i", h=HG),
                                                 block_max[:, half, :, :, 0:(half + 1) * CT], axis=AX.X, op=ALU.max,
                                                 negate=True))
                    m = HG * CT
                    if s:
                        wait_filled(dve, ("shift", s - 1))
                    link(nc.vector.tensor_copy(shift_parts[:, 0:m], neg_max[:, :]))
                    nc.vector.tensor_tensor(shift_parts[:, m:2 * m], neg_max[:, :], shift_parts[:, 0:m],
                                            ALU.subtract).then_inc(shift_split, 1)
                elif e[0] == "ot":
                    s, k = e[1], e[1] % 2
                    wait_filled(dve, e)
                    if s >= 2:
                        dve.wait_ge(attn_added, s - 1)
                    o = bank(e).rearrange("p (t h d) -> p t h d", t=CT, h=HG)
                    link(nc.vector.reciprocal(inv_sum[:, k, :, :], o[:, :, :, HEAD_DIM]))
                    ins = nc.vector.tensor_tensor(
                        attn[:, k, :, :, :], o[:, :, :, 0:HEAD_DIM],
                        inv_sum[:, k, :, :].unsqueeze(3).to_broadcast([P, CT, HG, HEAD_DIM]), ALU.mult)
                    drained(ins, e)
                elif e[0] == "scale":
                    c = e[1]
                    src, n = quant_blocks(c)
                    if c == "w":
                        dve.wait_ge(wffn_loaded, 16)
                    if quant_count[c] > 1:
                        dve.wait_ge(rounded, quant_count[c] - 1)
                    if c != "w" and c >= 2:
                        wait_drained(dve, ("ffn", c - 2, CT - 1))
                    link(nc.vector.tensor_reduce(amax[:, 0:n], src, axis=AX.X, op=ALU.max,
                                                 apply_absolute_value=True))
                    link(nc.vector.tensor_scalar(scales_of(c, n), amax[:, 0:n], 1.0 / FP8_MAX, None, ALU.mult))
                    nc.vector.reciprocal(qinv[:, 0:n], scales_of(c, n)).then_inc(scales_ready, 1)
                elif e[0] == "ffn":
                    _, c, t = e
                    n = ffn_count[c, t]
                    wait_filled(dve, e)
                    if n == 1:
                        wait_drained(dve, ("wscale",))
                        dve.wait_ge(second_rotated, len(splits))
                    if n > 4:
                        dve.wait_ge(ffn_added, n - 4)
                    dve.wait_ge(ffn_first, n)
                    drained(nc.vector.scalar_tensor_tensor(
                        ffn_sb[:, n % 4, EMBED:2 * EMBED], bank(e)[:, EMBED:2 * EMBED],
                        qscale[:, c % 2, t * EH + 1:t * EH + 2], w_scales[:, 1, :], ALU.mult, ALU.mult), e)
                elif e[0] == "expo":
                    c = e[1]
                    v, n = quant_blocks(c)
                    dve.wait_ge(scaled_ready, quant_count[c])
                    link(nc.vector.tensor_scalar(qexp[:, 0:n, :].bitcast(U32), v.bitcast(U32), 0x7F800000,
                                                 None, ALU.bitwise_and))
                    nc.vector.tensor_scalar(qexp[:, 0:n, :], qexp[:, 0:n, :], FP8_LEAST_NORMAL, ROUND_3_BITS,
                                            ALU.max, ALU.mult).then_inc(exponents_ready, 1)

        @block.tensor
        def _(pe):
            pe.wait_ge(consts_set, 1)
            pe.wait_ge(psum_cleared, 1)
            for e in order:
                if e[0] == "xt":
                    _, c, eh = e
                    pe.wait_ge(xn_ready, chunk_count[c])
                    wait_free(pe, e)
                    for t in range(CT):
                        ins = nc.tensor.transpose(bank(e)[:, t * P:(t + 1) * P],
                                                  xn[:, c * CT + t, eh * P:(eh + 1) * P], ident[:, :])
                    filled(ins, e)
                elif e[0] == "ckv":
                    c = e[1]
                    for eh in range(EH):
                        wait_drained(pe, ("xt", c, eh))
                    if c == 0:
                        pe.wait_ge(w_loaded, 48)
                    wait_free(pe, e)
                    for eh in range(EH):
                        ins = nc.tensor.matmul(bank(e)[0:LATENT, :], wkd_sb[:, eh, :], xnt[:, c % 2, eh, :],
                                               start=(eh == 0), stop=(eh == EH - 1))
                    filled(ins, e)
                elif e[0] == "proj":
                    _, t, c, ab = e
                    wait_free(pe, e)
                    if t == 0:
                        if c == 0:
                            pe.wait_ge(wq_loaded, 16)
                        for eh in range(EH):
                            wait_drained(pe, ("xt", c, eh))
                            ins = nc.tensor.matmul(bank(e), wq_sb[:, eh, ab * P:(ab + 1) * P],
                                                   xnt[:, c % 2, eh, :], start=(eh == 0), stop=(eh == EH - 1))
                    else:
                        wait_drained(pe, ("ckv", c))
                        ins = nc.tensor.matmul(bank(e), wku_sb[:, ab * P:(ab + 1) * P], ckvt[:, c % 2, :],
                                               start=True, stop=True)
                    filled(ins, e)
                elif e[0] == "v":
                    _, c, pair = e
                    wait_drained(pe, ("ckv", c))
                    wait_free(pe, e)
                    for t in range(2):
                        tok = (2 * pair + t) * P
                        ins = nc.tensor.matmul(bank(e)[:, t * EMBED:(t + 1) * EMBED], ckvt[:, c % 2, tok:tok + P],
                                               wv_sb[:, :], start=True, stop=True)
                    filled(ins, e)
                elif e[0] == "s":
                    _, s, u = e
                    if u == 0:
                        pe.wait_ge(kq_loaded[s % KQ_SLOTS], 16 * 2 * LOADS * (s // KQ_SLOTS + 1))
                    wait_free(pe, e)
                    half, k = half_of(s), s % KQ_SLOTS
                    unit = UNITS[half][u]
                    first, col = True, 0
                    for h, i, j, n in unit:
                        if j <= i < j + n and not (n == 1 and col):
                            at0 = col + (i - j) * P
                            w = 4 * P if n == 1 else P
                            nc.tensor.matmul(bank(e)[:, at0:at0 + w], ident_bf[:, :],
                                             mask_bf[:, 0:w // P, :].rearrange("p a n -> p (a n)"),
                                             start=first, stop=False, skip_group_check=True)
                            first = False
                        col += n * P
                    col = 0
                    for h, i, j, n in unit:
                        q0, k0 = (i - half * CT) * P, j % CT * P
                        ins = nc.tensor.matmul(bank(e)[:, col:col + n * P], qt[0:SPLIT_ROWS, k, h, q0:q0 + P],
                                               kt[0:SPLIT_ROWS, k, j // CT, h, k0:k0 + n * P], start=first, stop=True,
                                               skip_group_check=True)
                        first = False
                        col += n * P
                    filled(ins, e)
                elif e[0] == "shift":
                    pe.wait_ge(shift_split, e[1] + 1)
                    wait_free(pe, e)
                    n = 2 * HG * CT
                    filled(nc.tensor.transpose(bank(e)[0:n, 0:P // 2].bitcast(BF16), shift_parts[:, :],
                                               ident_bf[:, :]), e)
                elif e[0] == "t":
                    _, s, q, u = e
                    if q == 0 and u == 0:
                        pe.wait_ge(shift_placed, 32 * (s + 1))
                    wait_free(pe, e)
                    half, k, col = half_of(s), s % KQ_SLOTS, 0
                    segments, heads = QUADS[half][q]
                    for h in range(u * heads, (u + 1) * heads):
                        for j, q0, n in segments:
                            c0, k0 = (q0 - half * CT) * P, j % CT * P
                            ins = nc.tensor.matmul(bank(e)[:, col:col + n * P], kt[:, k, j // CT, h, k0:k0 + P],
                                                   qt[:, k, h, c0:c0 + n * P], start=True, stop=True)
                            col += n * P
                    filled(ins, e)
                elif e[0] == "pv":
                    _, s, q = e
                    c, g = STAGES[s]
                    half, n = c % CPB, quads[s, q]
                    segments = QUADS[half][q][0]
                    wait_drained(pe, last_unit[s, q])
                    if diagonals(half, q):
                        pe.wait_ge(probs_zeroed, diag_count[s, q])
                    if q == 0:
                        wait_free(pe, ("o", s))
                    col = 0
                    for j, q0, w in segments:
                        c0 = (q0 - half * CT) * P
                        for h in range(HG):
                            ins = nc.tensor.matmul(
                                ps[32 * h:32 * h + VC, BANK_O, c0:c0 + w * P],
                                v_sb[:, c // CPB, j, g * HG + h, :],
                                probs[:, n % PR, h, col:col + w * P],
                                start=(q == 0), stop=(q == len(QUADS[half]) - 1), skip_group_check=True)
                        col += w * P
                    ins.then_inc(pv_done, 1)
                elif e[0] == "ot":
                    s = e[1]
                    wait_drained(pe, ("o", s))
                    wait_free(pe, e)
                    for t in range(CT):
                        ins = nc.tensor.transpose(bank(e)[:, t * P:(t + 1) * P], o_sb[:, s % 2, t * P:(t + 1) * P],
                                                  ident[:, :])
                    filled(ins, e)
                elif e[0] in ("xdt", "wt"):
                    c = "w" if e[0] == "wt" else e[1]
                    m, tiles = quant_count[c], EH if c == "w" else CT
                    pe.wait_ge(rounded, m)
                    wait_free(pe, e)
                    to = bank(e)[:, 0:EH * tiles * P // 2].bitcast(BF16)
                    for k in range(EH):
                        for t in range(tiles):
                            ins = nc.tensor.transpose(to[:, (k * tiles + t) * P:(k * tiles + t + 1) * P],
                                                      quantized[:, m % 2, t * EH + k, :], ident_bf[:, :])
                    filled(ins, e)
                elif e[0] == "wscale":
                    pe.wait_ge(scales_ready, quant_count["w"])
                    wait_free(pe, e)
                    for k in range(EH):
                        for a in range(EH):
                            ins = nc.tensor.matmul(bank(e)[:, (k * EH + a) * P:(k * EH + a + 1) * P],
                                                   qscale[:, 2, a * EH + k:a * EH + k + 1].to_broadcast([P, P]),
                                                   ident[:, :], start=True, stop=True)
                    filled(ins, e)
                elif e[0] == "ffn":
                    _, c, t = e
                    wait_drained(pe, ("xdt", c))
                    wait_drained(pe, ("wt",))
                    wait_free(pe, e)
                    for k in range(EH):
                        ins = nc.tensor.matmul(bank(e)[:, k * EMBED:(k + 1) * EMBED], xdt(c)[:, k, t * P:(t + 1) * P],
                                               wt[:, k, :], start=True, stop=True)
                    filled(ins, e)


def rope_tables():
    import numpy as np
    freqs = np.float32(1.0) / np.power(np.float32(THETA), np.arange(0, ROPE, 2, dtype=np.float32) / np.float32(ROPE))
    angle = freqs.astype(np.float32)[:, None] * np.arange(SEQ, dtype=np.float32)[None, :]
    still = np.zeros((NOPE // 2, SEQ), np.float32)
    angle = np.concatenate([still, angle]).astype(np.float32)
    return np.cos(angle).astype(np.float32), np.sin(angle).astype(np.float32)


def column_order():
    first = list(range(NOPE // 2)) + list(range(NOPE, HEAD_DIM, 2))
    second = list(range(NOPE // 2, NOPE)) + list(range(NOPE + 1, HEAD_DIM, 2))
    return [h * HEAD_DIM + d for dims in (first, second) for d in dims for h in range(HEADS)]


def kernel(**inputs):
    import numpy as np
    import concourse.bacc as bacc
    from concourse.bass_utils import run_bass_kernel_spmd

    cos, sin = rope_tables()
    cols = column_order()
    arrays = {
        "x": np.ascontiguousarray(inputs["L0_attn_x"]),
        "wq": np.ascontiguousarray(np.asarray(inputs["L0_attn_Wq"])[:, cols]),
        "wkd": np.ascontiguousarray(inputs["L0_attn_Wkv_down"]),
        "wku": np.ascontiguousarray(np.asarray(inputs["L0_attn_Wk_up"])[:, cols]),
        "wv": np.ascontiguousarray(inputs["L0_attn_Wv_up"]),
        "wffn": np.ascontiguousarray(inputs["L0_ffn_weight"]),
        "cos": cos,
        "sin": sin,
    }
    nc = bacc.Bacc("TRN2", target_bir_lowering=False, num_devices=1)
    aps = {n: nc.dram_tensor(n, a.shape, mybir.dt.from_np(a.dtype), kind="ExternalInput").ap()
           for n, a in arrays.items()}
    out = nc.dram_tensor("out", (BATCH, SEQ, EMBED), F32, kind="ExternalOutput").ap()
    build(nc, *aps.values(), out)
    r = run_bass_kernel_spmd(nc, [arrays], core_ids=[0])
    return r.results[0]["out"]
```
